# Optimizing a Trainium2 kernel written in Bass

```python
import numpy as np
import jax
import jax.numpy as jnp

def _softmax(x, axis=-1):
    return jax.nn.softmax(x, axis=axis)

def _gelu(x):
    return jax.nn.gelu(x, approximate=True)

def _silu(x):
    return jax.nn.silu(x)

def _sigmoid(x):
    return jax.nn.sigmoid(x)

def _layernorm(x, axis=-1, eps=1e-05):
    m = jnp.mean(x, axis=axis, keepdims=True)
    v = jnp.var(x, axis=axis, keepdims=True)
    return (x - m) / jnp.sqrt(v + eps)

def _scatter_add(tgt, idx, src, axis=0):
    return tgt.at[idx].add(src)

def _segment_sum(src, seg, n):
    return jax.ops.segment_sum(src, seg, n)
kernel_name = 'mk_xattn_seq_d1_seqx_r4_1e631f'

def setup_inputs(seed: int=0):
    np.random.seed(seed)
    _w = jnp.asarray

    def _rec_inputs():
        import jax
        import jax.numpy as jnp
        _rk = jax.random.key(seed)
        x = 7.22e-05 + 1 * jax.random.normal(jax.random.fold_in(_rk, 1), (32, 256, 256), jnp.float32)
        _lenS = 256 - jax.random.randint(jax.random.fold_in(_rk, 7), (32,), 0, max(1, 256 // 4) + 1, jnp.int32)
        _lenS2 = 256 - jax.random.randint(jax.random.fold_in(_rk, 8), (32,), 0, max(1, 256 // 4) + 1, jnp.int32)
        _ctx_768P = jax.random.normal(jax.random.fold_in(_rk, 11), (32, 16, 192), jnp.float32)
        _ctx_768c = jax.random.dirichlet(jax.random.fold_in(_rk, 511), 0.3 * jnp.ones((16,), jnp.float32), (32, 256))
        _ctx_768t = jnp.einsum('bsk,bkd->bsd', _ctx_768c, _ctx_768P)
        _ctx_768t = _ctx_768t * jax.lax.rsqrt(jnp.mean(jnp.square(_ctx_768t)) + 1e-12) * 0.953939
        ctx_768 = -0.00055796 + 0.999787 * (_ctx_768t + 0.3 * jax.random.normal(jax.random.fold_in(_rk, 611), (32, 256, 192), jnp.float32))
        return (x, ctx_768)
    x, ctx_768 = _rec_inputs()

    def _L0_xattn_setup():
        import jax, jax.numpy as jnp
        import numpy as np
        D_MODEL = 256
        D_COND = 192
        N_HEADS = 16
        D_HEAD = 64
        D_ATTN = N_HEADS * D_HEAD
        D_FF = 4 * D_MODEL

        def _layernorm(x, g, b, eps=1e-05):
            mu = jnp.mean(x, axis=-1, keepdims=True)
            var = jnp.var(x, axis=-1, keepdims=True)
            return (x - mu) * jax.lax.rsqrt(var + eps) * g + b

        def _attention(xq, xkv, wq, wk, wv, wo, bo):
            B, S, _ = xq.shape
            T = xkv.shape[1]
            q = (xq @ wq).reshape(B, S, N_HEADS, D_HEAD)
            k = (xkv @ wk).reshape(B, T, N_HEADS, D_HEAD)
            v = (xkv @ wv).reshape(B, T, N_HEADS, D_HEAD)
            scale = D_HEAD ** (-0.5)
            attn = jnp.einsum('bihd,bjhd->bhij', q, k) * scale
            attn = jax.nn.softmax(attn, axis=-1)
            out = jnp.einsum('bhij,bjhd->bihd', attn, v).reshape(B, S, D_ATTN)
            return out @ wo + bo
        key = jax.random.key(seed)
        ks = jax.random.split(key, 16)
        B, S, T = (8, 256, 64)
        n = jax.random.normal
        inp = {'x': n(ks[0], (B, S, D_MODEL), jnp.float32), 'cond_emb': n(ks[1], (B, T, D_COND), jnp.float32), 'ln1_g': jnp.ones((D_MODEL,), jnp.float32), 'ln1_b': jnp.zeros((D_MODEL,), jnp.float32), 'ln2_g': jnp.ones((D_MODEL,), jnp.float32), 'ln2_b': jnp.zeros((D_MODEL,), jnp.float32), 'ln3_g': jnp.ones((D_MODEL,), jnp.float32), 'ln3_b': jnp.zeros((D_MODEL,), jnp.float32), 'sa_wq': n(ks[2], (D_MODEL, D_ATTN), jnp.float32) * D_MODEL ** (-0.5), 'sa_wk': n(ks[3], (D_MODEL, D_ATTN), jnp.float32) * D_MODEL ** (-0.5), 'sa_wv': n(ks[4], (D_MODEL, D_ATTN), jnp.float32) * D_MODEL ** (-0.5), 'sa_wo': n(ks[5], (D_ATTN, D_MODEL), jnp.float32) * D_ATTN ** (-0.5), 'sa_bo': jnp.zeros((D_MODEL,), jnp.float32), 'ca_wq': n(ks[6], (D_MODEL, D_ATTN), jnp.float32) * D_MODEL ** (-0.5), 'ca_wk': n(ks[7], (D_COND, D_ATTN), jnp.float32) * D_COND ** (-0.5), 'ca_wv': n(ks[8], (D_COND, D_ATTN), jnp.float32) * D_COND ** (-0.5), 'ca_wo': n(ks[9], (D_ATTN, D_MODEL), jnp.float32) * D_ATTN ** (-0.5), 'ca_bo': jnp.zeros((D_MODEL,), jnp.float32), 'ff_w1': n(ks[10], (D_MODEL, 2 * D_FF), jnp.float32) * D_MODEL ** (-0.5), 'ff_b1': jnp.zeros((2 * D_FF,), jnp.float32), 'ff_w2': n(ks[11], (D_FF, D_MODEL), jnp.float32) * D_FF ** (-0.5), 'ff_b2': jnp.zeros((D_MODEL,), jnp.float32)}
        return inp
    _L0_xattn_all = _L0_xattn_setup()
    _L0_xattn_in = {k: v for k, v in _L0_xattn_all.items() if k in ('ln1_g', 'ln1_b', 'ln2_g', 'ln2_b', 'ln3_g', 'ln3_b', 'sa_wq', 'sa_wk', 'sa_wv', 'sa_wo', 'sa_bo', 'ca_wq', 'ca_wk', 'ca_wv', 'ca_wo', 'ca_bo', 'ff_w1', 'ff_b1', 'ff_w2', 'ff_b2')}
    del _L0_xattn_all
    return {'x': x, 'ctx_768': ctx_768, 'L0_xattn_ln1_g': _L0_xattn_in['ln1_g'], 'L0_xattn_ln1_b': _L0_xattn_in['ln1_b'], 'L0_xattn_ln2_g': _L0_xattn_in['ln2_g'], 'L0_xattn_ln2_b': _L0_xattn_in['ln2_b'], 'L0_xattn_ln3_g': _L0_xattn_in['ln3_g'], 'L0_xattn_ln3_b': _L0_xattn_in['ln3_b'], 'L0_xattn_sa_wq': _L0_xattn_in['sa_wq'], 'L0_xattn_sa_wk': _L0_xattn_in['sa_wk'], 'L0_xattn_sa_wv': _L0_xattn_in['sa_wv'], 'L0_xattn_sa_wo': _L0_xattn_in['sa_wo'], 'L0_xattn_sa_bo': _L0_xattn_in['sa_bo'], 'L0_xattn_ca_wq': _L0_xattn_in['ca_wq'], 'L0_xattn_ca_wk': _L0_xattn_in['ca_wk'], 'L0_xattn_ca_wv': _L0_xattn_in['ca_wv'], 'L0_xattn_ca_wo': _L0_xattn_in['ca_wo'], 'L0_xattn_ca_bo': _L0_xattn_in['ca_bo'], 'L0_xattn_ff_w1': _L0_xattn_in['ff_w1'], 'L0_xattn_ff_b1': _L0_xattn_in['ff_b1'], 'L0_xattn_ff_w2': _L0_xattn_in['ff_w2'], 'L0_xattn_ff_b2': _L0_xattn_in['ff_b2']}

def reference(x, ctx_768, L0_xattn_ln1_g, L0_xattn_ln1_b, L0_xattn_ln2_g, L0_xattn_ln2_b, L0_xattn_ln3_g, L0_xattn_ln3_b, L0_xattn_sa_wq, L0_xattn_sa_wk, L0_xattn_sa_wv, L0_xattn_sa_wo, L0_xattn_sa_bo, L0_xattn_ca_wq, L0_xattn_ca_wk, L0_xattn_ca_wv, L0_xattn_ca_wo, L0_xattn_ca_bo, L0_xattn_ff_w1, L0_xattn_ff_b1, L0_xattn_ff_w2, L0_xattn_ff_b2):
    import jax
    import jax.numpy as jnp

    def _L0_xattn_ref(x, cond_emb, ln1_g, ln1_b, ln2_g, ln2_b, ln3_g, ln3_b, sa_wq, sa_wk, sa_wv, sa_wo, sa_bo, ca_wq, ca_wk, ca_wv, ca_wo, ca_bo, ff_w1, ff_b1, ff_w2, ff_b2):
        import jax, jax.numpy as jnp
        import numpy as np
        D_MODEL = 256
        D_COND = 192
        N_HEADS = 16
        D_HEAD = 64
        D_ATTN = N_HEADS * D_HEAD
        D_FF = 4 * D_MODEL

        def _layernorm(x, g, b, eps=1e-05):
            mu = jnp.mean(x, axis=-1, keepdims=True)
            var = jnp.var(x, axis=-1, keepdims=True)
            return (x - mu) * jax.lax.rsqrt(var + eps) * g + b

        def _attention(xq, xkv, wq, wk, wv, wo, bo):
            B, S, _ = xq.shape
            T = xkv.shape[1]
            q = (xq @ wq).reshape(B, S, N_HEADS, D_HEAD)
            k = (xkv @ wk).reshape(B, T, N_HEADS, D_HEAD)
            v = (xkv @ wv).reshape(B, T, N_HEADS, D_HEAD)
            scale = D_HEAD ** (-0.5)
            attn = jnp.einsum('bihd,bjhd->bhij', q, k) * scale
            attn = jax.nn.softmax(attn, axis=-1)
            out = jnp.einsum('bhij,bjhd->bihd', attn, v).reshape(B, S, D_ATTN)
            return out @ wo + bo
        h = _layernorm(x, ln1_g, ln1_b)
        x = _attention(h, h, sa_wq, sa_wk, sa_wv, sa_wo, sa_bo) + x
        h = _layernorm(x, ln2_g, ln2_b)
        x = _attention(h, cond_emb, ca_wq, ca_wk, ca_wv, ca_wo, ca_bo) + x
        h = _layernorm(x, ln3_g, ln3_b)
        p = h @ ff_w1 + ff_b1
        a, gate = (p[..., :D_FF], p[..., D_FF:])
        h = a * jax.nn.gelu(gate, approximate=False) @ ff_w2 + ff_b2
        return h + x
    x = _L0_xattn_ref(x, ctx_768, L0_xattn_ln1_g, L0_xattn_ln1_b, L0_xattn_ln2_g, L0_xattn_ln2_b, L0_xattn_ln3_g, L0_xattn_ln3_b, L0_xattn_sa_wq, L0_xattn_sa_wk, L0_xattn_sa_wv, L0_xattn_sa_wo, L0_xattn_sa_bo, L0_xattn_ca_wq, L0_xattn_ca_wk, L0_xattn_ca_wv, L0_xattn_ca_wo, L0_xattn_ca_bo, L0_xattn_ff_w1, L0_xattn_ff_b1, L0_xattn_ff_w2, L0_xattn_ff_b2)
    return x

_drawn_inputs = setup_inputs


def setup_inputs(seed=0):
    import zlib

    import numpy as np

    out = dict(_drawn_inputs(seed))
    spreads = {'L0_xattn_ln1_g': (1.0, 0.2),
     'L0_xattn_ln1_b': (0.0, 0.1),
     'L0_xattn_ln2_g': (1.0, 0.2),
     'L0_xattn_ln2_b': (0.0, 0.356),
     'L0_xattn_ln3_g': (1.0, 0.2),
     'L0_xattn_ln3_b': (0.0, 0.1),
     'L0_xattn_sa_bo': (0.0, 0.1),
     'L0_xattn_ca_bo': (0.0, 0.1),
     'L0_xattn_ff_b1': (0.0, 0.1),
     'L0_xattn_ff_b2': (0.0, 0.1)}
    factors = {}
    for name, (base, spread) in spreads.items():
        noise = np.random.default_rng([zlib.crc32(name.encode()), seed]).standard_normal(out[name].shape)
        drawn = base * np.exp(spread * noise) if base else spread * noise
        out[name] = jnp.asarray(drawn.astype(out[name].dtype))
    for name, factor in factors.items():
        out[name] = (out[name] * factor).astype(out[name].dtype)
    return out
```

```python
from contextlib import ExitStack

import concourse.bass as bass
from concourse import mybir

F32 = mybir.dt.float32
F32R = mybir.dt.float32r
ALU = mybir.AluOpType
ACT = mybir.ActivationFunctionType
AX_X = mybir.AxisListType.X

P = 128
D = 256
DK = D // P
S = 256
IT = S // P
H = 16
DH = 64
DA = H * DH
PAIRS = H // 2
HALF = PAIRS // 2
EPS = 1e-5
SCALE = DH ** -0.5
DFF = 4 * D
FT = DFF // P
WCOLS = 2048
FILL, START, STEADY, LAST, DRAIN = ("nxt",), ("cur", "nxt"), ("prv", "cur", "nxt"), ("prv", "cur"), ("prv",)
LEFT, RIGHT = slice(0, DH), slice(DH, 2 * DH)


class Slots:

    def __init__(self, x_units, batches):
        order = []
        for m in range(PAIRS):
            order += [(u, part) for u, part in f1_units(m, x_units)]
        self.order, self.batches = order, batches
        self.before_loop = self._size(FILL) + self._size(START)
        self.total = self.before_loop + (batches - 2) * len(order) + self._size(LAST) + self._size(DRAIN)

    def _size(self, parts):
        return sum(part in parts for _, part in self.order)

    def through(self, t, unit, parts):
        place = 1 + [u for u, part in self.order if part in parts].index(unit)
        if isinstance(t, int) and t < 1:
            return place + (self._size(FILL) if t == 0 else 0)
        if isinstance(t, int) and t == self.batches:
            return self.total - self._size(DRAIN) + place
        return (t - 1) * len(self.order) + self.before_loop + place


def f1_units(m, x_units):
    early = [(("wo", 0, 0), "prv"), (("wo", 0, 1), "prv"), (("o", 7), "prv"), (("v", 1, 1), "cur"),
             (("wo", 1, 0), "prv"), (("wo", 1, 1), "prv"), (("o", 3), "cur"), (("v", 0, 1), "nxt")][m]
    late = [(("o", 5), "prv"), (("o", 6), "prv"), (("v", 1, 0), "cur"), (("o", 0), "cur"),
            (("o", 1), "cur"), (("o", 2), "cur"), (("v", 0, 0), "nxt"), (("o", 4), "cur")][m]
    return [early, late] + ([(("x", k), "nxt") for k in range(x_units)] if m == 3 else [])


def heads_split(m):
    return [[(4, "prv")], [(5, "prv")], [(6, "prv"), (7, "prv")], [], [(0, "cur")], [(1, "cur")], [(2, "cur"), (3, "cur")], []][m]


def batch_of(t, part):
    return t - 1 if part == "prv" else t if part == "cur" else t + 1


def at_least(eng, sem, value):
    if not (isinstance(value, int) and value <= 0):
        eng.wait_ge(sem, value)


def over_batches(eng, batches, iteration, unroll=1):
    iteration(-1, FILL, 1)
    iteration(0, START, 0)
    with eng.Fori(1, batches - unroll, unroll) as t:
        for i in range(unroll):
            iteration(t + i if i else t, STEADY, (1 + i) % 2)
    iteration(batches - 1, LAST, 1)
    iteration(batches, DRAIN, 0)


def block_kernel(nc, x, ctx, ln1_g, ln1_b, ln2_g, ln2_b, ln3_g, ln3_b, sa_wq, sa_wk, sa_wv, sa_wo, sa_bo,
                 ca_wq, ca_wk, ca_wv, ca_wo, ca_bo, ff_w1, ff_b1, ff_w2, ff_b2, out):
    B = x.shape[0]
    DC = ctx.shape[2]
    stack = ExitStack()
    with stack:
        def sb(name, shape, dt=F32):
            return stack.enter_context(nc.sbuf_tensor(name, shape, dt))

        def psum(name, shape):
            return stack.enter_context(nc.psum_tensor(name, shape, F32))

        def sem(name):
            return stack.enter_context(nc.semaphore(name))

        x_sa = nc.dram_tensor("x_sa_dram", (B, S, D), F32).ap()
        x_ca = nc.dram_tensor("x_ca_dram", (B, S, D), F32).ap()

        s_ps = psum("s_ps", [P, 2, 2, IT * S])
        pt_ps = psum("pt_ps", [P, 2, 2 * S])
        f0_ps = psum("f0_ps", [P, 2 * S])
        f1_ps = psum("f1_ps", [P, 2 * S])

        w_hi = sb("w_hi", [P, 4, WCOLS], F32R)
        w_lo = sb("w_lo", [P, 4, WCOLS], F32R)
        w_stage = sb("w_stage", [P, 2, WCOLS])
        ln_gb = sb("ln_gb", [P, 3, 2, DK])
        b1_col = sb("b1_col", [P, 2 * FT])
        out_bias = sb("out_bias", [P, 3, D])
        ident = sb("ident", [P, P])
        neg_half = sb("neg_half", [P, IT])
        eps = sb("eps", [P, IT])

        x_ln = sb("x_ln", [P, IT, D])
        x_n = sb("x_n", [P, IT, D])
        ctx_in = sb("ctx_in", [P, IT, DK * P])
        x_res = sb("x_res", [P, IT, D])
        x_rb = sb("x_rb", [P, IT, D])
        x_out = sb("x_out", [P, IT, D])
        bn = sb("bn", [P, IT, 6])
        mean_var = sb("mean_var", [P, IT, 2])
        var_eps = sb("var_eps", [P, IT])
        rstd = sb("rstd", [P, IT])
        hT_full = sb("hT_full", [P, 2, DK, S])
        hT_hi = sb("hT_hi", [P, 2, DK, S], F32R)
        hT_lo = sb("hT_lo", [P, 2, DK, S], F32R)
        qk_hi = sb("qk_hi", [P, PAIRS, 2, S], F32R)
        qk_lo = sb("qk_lo", [P, PAIRS, 2, S], F32R)
        v_hl = sb("v_hl", [P, IT, H, 2 * DH], F32R)
        probs = sb("probs", [P, 2, 2 * IT, S])
        neg_max = sb("neg_max", [P, 2, 2 * IT])
        row_sum = sb("row_sum", [P, 2, 2 * IT])
        row_inv = sb("row_inv", [P, 2, 2 * IT])
        pT_hi = sb("pT_hi", [P, 2, 2, 2 * S], F32R)
        pT_lo = sb("pT_lo", [P, 2, 2, 2 * S], F32R)
        o_lo = sb("o_lo", [DH, 2 * S])
        o_sum = sb("o_sum", [P, 2, S])
        a_hi = sb("a_hi", [P, PAIRS, S], F32R)
        a_lo = sb("a_lo", [P, PAIRS, S], F32R)
        gate = sb("gate", [P, 2, S])
        hid = sb("hid", [P, 2, S])

        const_ready = sem("const_ready")
        ident_zero = sem("ident_zero")
        param_ld = sem("param_ld")
        stage_ld = [sem("stage_ld0"), sem("stage_ld1")]
        w_hi_done = sem("w_hi_done")
        w_done = sem("w_done")

        class NormSemaphores:

            def __init__(self, name):
                self.x_ld = sem(f"{name}_x_ld")
                self.res_ld = sem(f"{name}_res_ld")
                self.stored = sem(f"{name}_stored")
                self.bn_done = sem(f"{name}_bn_done")
                self.stats_done = sem(f"{name}_stats_done")
                self.eps_done = sem(f"{name}_eps_done")
                self.rstd_ready = sem(f"{name}_rstd_ready")
                self.ln_done = sem(f"{name}_ln_done")
                self.x_full = sem(f"{name}_x_full")
                self.x_hi = sem(f"{name}_x_hi")
                self.x_lo = sem(f"{name}_x_lo")
                self.xrb_done = sem(f"{name}_xrb_done")

        class AttentionPass(NormSemaphores):

            def __init__(self, name, norm, x_in, x_to, ctx_rows, weights, w0, before):
                super().__init__(name)
                self.norm, self.x_in, self.x_to, self.weights, self.w0, self.before = norm, x_in, x_to, weights, w0, before
                self.kv = 1 if ctx_rows else 0
                self.kv_rows = ctx_rows or [P] * DK
                self.x_units = DK * (2 if ctx_rows else 1)
                self.slots = Slots(self.x_units, B)
                self.ctx_ld = sem(f"{name}_ctx_ld")
                self.qk_full = sem(f"{name}_qk_full")
                self.qk_hi = sem(f"{name}_qk_hi")
                self.qk_lo = sem(f"{name}_qk_lo")
                self.v_full = sem(f"{name}_v_full")
                self.v_hi = sem(f"{name}_v_hi")
                self.s_full = sem(f"{name}_s_full")
                self.max_done = sem(f"{name}_max_done")
                self.exp_done = sem(f"{name}_exp_done")
                self.inv_done = sem(f"{name}_inv_done")
                self.norm_done = sem(f"{name}_norm_done")
                self.pt_full = sem(f"{name}_pt_full")
                self.pt_hi = sem(f"{name}_pt_hi")
                self.pt_lo = sem(f"{name}_pt_lo")
                self.o_full = sem(f"{name}_o_full")
                self.o_bot = sem(f"{name}_o_bot")
                self.a_hi_done = sem(f"{name}_a_hi_done")
                self.a_done = sem(f"{name}_a_done")
                self.wo_full = sem(f"{name}_wo_full")
                self.f1_done = sem(f"{name}_f1_done")

        class FeedForwardPass(NormSemaphores):
            def __init__(self, name):
                super().__init__(name)
                self.x_mid = sem(f"{name}_x_mid")
                self.p_full = sem(f"{name}_p_full")
                self.gate_done = sem(f"{name}_gate_done")
                self.hid_done = sem(f"{name}_hid_done")
                self.u_hi = sem(f"{name}_u_hi")
                self.u_lo = sem(f"{name}_u_lo")
                self.w2_full = sem(f"{name}_w2_full")
                self.y_done = sem(f"{name}_y_done")

        sa = AttentionPass("sa", 0, x, x_sa, None, [(sa_wq, SCALE), (sa_wk, 1.0), (sa_wv, 1.0), (sa_wo, 1.0)], 0, None)
        ca = AttentionPass("ca", 1, x_sa, x_ca, [P, DC - P], [(ca_wq, SCALE), (ca_wk, 1.0), (ca_wv, 1.0), (ca_wo, 1.0)], 4, sa)
        ff = FeedForwardPass("ff")
        passes = (sa, ca)

        w1_v = ff_w1.rearrange("(k p) n -> p k n", p=P)
        staged = [(w, scale, slot) for ph in passes for slot, (w, scale) in enumerate(ph.weights)]
        staged += [(w1_v[:, 0, :], 1.0, 0), (w1_v[:, 1, :], 1.0, 1), (ff_w2, 1.0, 2)]

        def w_pieces(n):
            w = staged[n][0]
            if w.shape[0] == P:
                return [(w, P, slice(0, WCOLS))]
            if w.shape[0] % P:
                cols = w.shape[1]
                return [(w[0:P, :], P, slice(0, cols)), (w[P:, :], w.shape[0] - P, slice(cols, 2 * cols))]
            return [(w.rearrange("(k p) n -> p k n", p=P), P, slice(0, WCOLS))]

        def tiles(a):
            return a.rearrange("(i p) d -> p i d", p=P)

        def f32(a):
            return a.bitcast(F32)

        block = stack.enter_context(nc.Block())

        @block.sync
        def _(sp):
            def load_weight(n):
                if n >= 2:
                    sp.wait_ge(w_done, n - 1)
                for w, rows, cols in w_pieces(n):
                    dst = w_stage[0:rows, n % 2, cols]
                    if len(w.shape) == 3:
                        dst = dst.rearrange("p (k n) -> p k n", k=w.shape[1])
                    sp.dma_start(dst, w).then_inc(stage_ld[n % 2], 16)

            def attention(ph):
                def iteration(t, parts, _parity):
                    if "nxt" in parts:
                        at_least(sp, ph.ln_done, t + 1)
                        sp.dma_start(x_ln[:], tiles(ph.x_in[t + 1])).then_inc(ph.x_ld, 16)
                        if ph.kv:
                            at_least(sp, ph.x_full, ph.x_units * (t + 1))
                            sp.dma_start(ctx_in[:, :, 0:DC], tiles(ctx[t + 1])).then_inc(ph.ctx_ld, 16)
                    if parts == FILL:
                        for n in range(4):
                            load_weight(ph.w0 + n)
                    if "cur" in parts:
                        at_least(sp, ph.xrb_done, t)
                        sp.dma_start(x_res[:], tiles(ph.x_in[t])).then_inc(ph.res_ld, 16)
                    if "prv" in parts:
                        sp.wait_ge(ph.f1_done, ph.slots.through(t, ("wo", 1, 1), parts))
                        sp.dma_start(tiles(ph.x_to[t - 1]), x_out[:]).then_inc(ph.stored, 16)
                over_batches(sp, B, iteration)
                sp.wait_ge(ph.stored, 16 * B)

            for i, (g, b) in enumerate(((ln1_g, ln1_b), (ln2_g, ln2_b), (ln3_g, ln3_b))):
                sp.dma_start(ln_gb[:, i, 0, :], g.rearrange("(k p) -> p k", p=P),
                             allow_slow_non_contiguous=True).then_inc(param_ld, 16)
                sp.dma_start(ln_gb[:, i, 1, :], b.rearrange("(k p) -> p k", p=P),
                             allow_slow_non_contiguous=True).then_inc(param_ld, 16)
            sp.dma_start(b1_col[:], ff_b1.rearrange("(k p) -> p k", p=P),
                             allow_slow_non_contiguous=True).then_inc(param_ld, 16)
            for i, b in enumerate((sa_bo, ca_bo, ff_b2)):
                sp.dma_start(out_bias[:, i, :], b.unsqueeze(0).broadcast_to([P, D])).then_inc(param_ld, 16)
            for ph in passes:
                attention(ph)

            def iteration(t, parts, _parity):
                if "nxt" in parts:
                    at_least(sp, ff.ln_done, t + 1)
                    sp.dma_start(x_ln[:], tiles(x_ca[t + 1])).then_inc(ff.x_ld, 16)
                if parts == FILL:
                    for n in range(8, 11):
                        load_weight(n)
                if "cur" in parts:
                    at_least(sp, ff.xrb_done, t)
                    sp.dma_start(x_res[:], tiles(x_ca[t])).then_inc(ff.res_ld, 16)
                if "prv" in parts:
                    sp.wait_ge(ff.y_done, 2 * t)
                    sp.dma_start(tiles(out[t - 1]), x_out[:]).then_inc(ff.stored, 16)
            over_batches(sp, B, iteration, unroll=2)
            sp.wait_ge(ff.stored, 16 * B)

        @block.tensor
        def _(pe):
            def product(dst, pairs, start=True, stop=True):
                terms = [(a, b) for a_hi_, a_lo_, b_hi_, b_lo_ in pairs
                         for a, b in ((a_hi_, b_hi_), (a_hi_, b_lo_), (a_lo_, b_hi_))]
                for n, (a, b) in enumerate(terms):
                    last = nc.tensor.matmul(dst, a, b, start=start and n == 0, stop=stop and n == len(terms) - 1)
                return last

            def attention(ph):
                def scores(t, m):
                    g = t * PAIRS + m
                    pe.wait_ge(ph.qk_lo, g + 1)
                    at_least(pe, ph.exp_done, g - 1)
                    for it in range(IT):
                        rows = slice(it * P, (it + 1) * P)
                        for n, (q, k) in enumerate(((qk_hi, qk_hi), (qk_hi, qk_lo), (qk_lo, qk_hi))):
                            for hd, part in enumerate((LEFT, RIGHT)):
                                last = nc.tensor.matmul(s_ps[:, m % 2, hd, it * S:(it + 1) * S], q[part, m, 0, rows],
                                                        k[part, m, 1, :], start=n == 0, stop=n == 2)
                    last.then_inc(ph.s_full, 1)

                def transpose_probs(t, m):
                    g = t * PAIRS + m
                    pe.wait_ge(ph.norm_done, g + 1)
                    at_least(pe, ph.pt_lo, g)
                    for hd in range(2):
                        for jt in range(IT):
                            for it in range(IT):
                                last = nc.tensor.transpose(pt_ps[:, hd, jt * S + it * P:jt * S + (it + 1) * P],
                                                           probs[:, m % 2, hd * IT + it, jt * P:(jt + 1) * P], ident[:])
                    last.then_inc(ph.pt_full, 1)

                def project_qk(b, m):
                    if isinstance(b, int) and b == 0 and m == 0:
                        pe.wait_ge(w_done, ph.w0 + 2)
                    pe.wait_ge(ph.x_lo, ph.x_units * (b + 1))
                    at_least(pe, ph.qk_lo, b * PAIRS + m)
                    cols = [slice(k * DA + m * P, k * DA + (m + 1) * P) for k in range(DK)]
                    product(f0_ps[:, 0:S], [(w_hi[:, 0, cols[k]], w_lo[:, 0, cols[k]], hT_hi[:, 0, k, :], hT_lo[:, 0, k, :])
                                            for k in range(DK)])
                    product(f0_ps[:, S:2 * S],
                            [(w_hi[0:r, 1, cols[k]], w_lo[0:r, 1, cols[k]], hT_hi[0:r, ph.kv, k, :], hT_lo[0:r, ph.kv, k, :])
                             for k, r in enumerate(ph.kv_rows)]).then_inc(ph.qk_full, 1)

                def f1_unit(t, parts, unit, part):
                    b = batch_of(t, part)
                    at_least(pe, ph.f1_done, ph.slots.through(t, unit, parts) - 1)
                    if unit[0] == "wo":
                        _, half, it = unit
                        pe.wait_ge(ph.a_done, b * PAIRS + (half + 1) * HALF)
                        rows = slice(it * P, (it + 1) * P)
                        product(f1_ps[:, 0:D],
                                [(a_hi[:, m, rows], a_lo[:, m, rows], w_hi[:, 3, m * D:(m + 1) * D], w_lo[:, 3, m * D:(m + 1) * D])
                                 for m in range(half * HALF, (half + 1) * HALF)]).then_inc(ph.wo_full, 1)
                    elif unit[0] == "o":
                        m = unit[1]
                        pe.wait_ge(ph.pt_lo, b * PAIRS + m + 1)
                        for hd in range(2):
                            for n, (jt, pT) in enumerate((jt, pT) for jt in range(IT) for pT in (pT_hi, pT_lo)):
                                last = nc.tensor.matmul(f1_ps[:, hd * S:(hd + 1) * S], v_hl[:, jt, 2 * m + hd, :],
                                                        pT[:, m % 2, hd, jt * S:(jt + 1) * S], start=n == 0, stop=n == 3)
                        last.then_inc(ph.o_full, 1)
                    elif unit[0] == "v":
                        _, c, jt = unit
                        if isinstance(b, int) and b == 0 and c == 0 and jt == 0:
                            pe.wait_ge(w_done, ph.w0 + 3)
                        rows = slice(jt * P, (jt + 1) * P)
                        cols = [slice(k * DA + c * 2 * S, k * DA + (c + 1) * 2 * S) for k in range(DK)]
                        product(f1_ps[:],
                                [(hT_hi[0:r, ph.kv, k, rows], hT_lo[0:r, ph.kv, k, rows], w_hi[0:r, 2, cols[k]], w_lo[0:r, 2, cols[k]])
                                 for k, r in enumerate(ph.kv_rows)]).then_inc(ph.v_full, 1)
                    else:
                        k = unit[1]
                        if k == 0:
                            pe.wait_ge(ph.ln_done, b + 1)
                        elif k == DK:
                            pe.wait_ge(ph.ctx_ld, 16 * (b + 1))
                        src, k = (x_n, k) if k < DK else (ctx_in, k - DK)
                        for it in range(IT):
                            last = nc.tensor.transpose(f1_ps[:, it * P:(it + 1) * P], src[:, it, k * P:(k + 1) * P], ident[:])
                        last.then_inc(ph.x_full, 1)

                def iteration(t, parts, _parity):
                    if parts == START:
                        pe.wait_ge(w_done, ph.w0 + 4)
                    for m in range(PAIRS):
                        early, late, *xs = f1_units(m, ph.x_units)
                        if "cur" in parts:
                            scores(t, m)
                        if early[1] in parts:
                            f1_unit(t, parts, *early)
                        if m < 2 and "prv" in parts:
                            transpose_probs(t - 1, m + PAIRS - 2)
                        if m >= 2 and "cur" in parts:
                            transpose_probs(t, m - 2)
                        if m < HALF and "cur" in parts:
                            project_qk(t, m + HALF)
                        if m >= HALF and "nxt" in parts:
                            project_qk(t + 1, m - HALF)
                        if late[1] in parts:
                            f1_unit(t, parts, *late)
                        for unit in xs:
                            if unit[1] in parts:
                                f1_unit(t, parts, *unit)
                over_batches(pe, B, iteration)

            pe.wait_ge(const_ready, 4)
            for ph in passes:
                attention(ph)

            def hidden(t, m, parity):
                g = t * FT + m
                if m == 0:
                    pe.wait_ge(ff.x_lo, DK * (t + 1))
                at_least(pe, ff.hid_done, g - 3)
                for half in range(2):
                    cols = slice(half * DFF + m * P, half * DFF + (m + 1) * P)
                    last = product(s_ps[:, m % 4 // 2, m % 2, half * S:(half + 1) * S],
                                   [(w_hi[:, k, cols], w_lo[:, k, cols], hT_hi[:, parity, k, :], hT_lo[:, parity, k, :])
                                    for k in range(DK)])
                last.then_inc(ff.p_full, 1)

            def down(b, m):
                pe.wait_ge(ff.u_lo, b * FT + m + 1)
                if m == 0:
                    at_least(pe, ff.y_done, IT * b)
                for it, bank in enumerate((f0_ps, f1_ps)):
                    rows = slice(it * P, (it + 1) * P)
                    last = product(bank[:, 0:D], [(a_hi[:, m, rows], a_lo[:, m, rows],
                                                   w_hi[:, 2, m * D:(m + 1) * D], w_lo[:, 2, m * D:(m + 1) * D])],
                                   start=m == 0, stop=m == FT - 1)
                    if m == FT - 1:
                        last.then_inc(ff.w2_full, 1)

            def iteration(t, parts, parity):
                if parts == START:
                    pe.wait_ge(w_done, len(staged))
                for m in range(FT):
                    if "cur" in parts:
                        hidden(t, m, parity)
                    if m < 2 and "prv" in parts:
                        down(t - 1, m + FT - 2)
                    if m >= 2 and "cur" in parts:
                        down(t, m - 2)
                    if m == FT - 2 and "nxt" in parts:
                        pe.wait_ge(ff.ln_done, t + 2)
                        for k in range(DK):
                            at_least(pe, ff.x_mid, DK * (t + 1) + k - 1)
                            for it in range(IT):
                                last = nc.tensor.transpose(pt_ps[:, k, it * P:(it + 1) * P],
                                                           x_n[:, it, k * P:(k + 1) * P], ident[:])
                            last.then_inc(ff.x_full, 1)
            over_batches(pe, B, iteration, unroll=2)

        @block.scalar
        def _(act):
            def split_weight(n):
                pieces = w_pieces(n)
                if n < 2:
                    pass
                act.wait_ge(stage_ld[n % 2], 16 * sum(len(w_pieces(k)) for k in range(n % 2, n + 1, 2)))
                _, scale, slot = staged[n]
                for i, (_, rows, cols) in enumerate(pieces):
                    op = nc.scalar.activation(w_hi[0:rows, slot, cols], w_stage[0:rows, n % 2, cols], ACT.Copy, scale=scale)
                op.then_inc(w_hi_done, 1)

            def attention(ph):
                def split_probs(t, m):
                    act.wait_ge(ph.pt_full, t * PAIRS + m + 1)
                    nc.scalar.copy(pT_hi[:, m % 2, :, :], pt_ps[:]).then_inc(ph.pt_hi, 1)

                def split_heads(t, m, parts):
                    done = ph.slots.through(t, ("wo", 0, 0), parts) - 1 if m == HALF else ph.slots.through(t, ("o", m), parts)
                    act.wait_ge(ph.f1_done, done)
                    nc.scalar.copy(a_hi[:, m, :], o_sum[:, m % 2, :]).then_inc(ph.a_hi_done, 1)

                def exponentials(t, m):
                    act.wait_ge(ph.max_done, t * PAIRS + m + 1)
                    for r in range(2 * IT):
                        op = nc.scalar.activation(probs[:, m % 2, r, :], s_ps[:, m % 2, r // IT, r % IT * S:(r % IT + 1) * S],
                                                  ACT.Exp, bias=neg_max[:, m % 2, r:r + 1],
                                                  accum_out=row_sum[:, m % 2, r:r + 1])
                    op.then_inc(ph.exp_done, 1)

                def f1_unit(t, unit, part):
                    b = batch_of(t, part)
                    if unit[0] == "o":
                        act.wait_ge(ph.o_full, b * PAIRS + unit[1] + 1)
                        nc.scalar.copy(o_lo[:], f1_ps[DH:P, :]).then_inc(ph.o_bot, 1)
                    elif unit[0] == "v":
                        _, c, jt = unit
                        act.wait_ge(ph.v_full, 4 * b + 2 * c + jt + 1)
                        nc.scalar.copy(v_hl[:, jt, c * PAIRS:(c + 1) * PAIRS, LEFT],
                                       f1_ps[:].rearrange("p (h d) -> p h d", d=DH)).then_inc(ph.v_hi, 1)
                    elif unit[0] == "x":
                        k = unit[1]
                        act.wait_ge(ph.x_full, ph.x_units * b + k + 1)
                        if k < DK:
                            nc.scalar.activation(hT_hi[:, 0, k, :], f1_ps[:, 0:S], ACT.Identity,
                                                 scale=ln_gb[:, ph.norm, 0, k:k + 1],
                                                 bias=ln_gb[:, ph.norm, 1, k:k + 1]).then_inc(ph.x_hi, 1)
                        else:
                            rows = ph.kv_rows[k - DK]
                            nc.scalar.copy(hT_hi[0:rows, 1, k - DK, :], f1_ps[0:rows, 0:S]).then_inc(ph.x_hi, 1)

                def iteration(t, parts, _parity):
                    if parts == FILL:
                        if ph.before:
                            act.wait_ge(ph.before.f1_done, ph.before.slots.total)
                        for n in range(4):
                            split_weight(ph.w0 + n)
                    for m in range(PAIRS):
                        early, late, *xs = f1_units(m, ph.x_units)
                        if early[1] in parts:
                            f1_unit(t, *early)
                        if m < 2 and "prv" in parts:
                            split_probs(t - 1, m + PAIRS - 2)
                        if m >= 2 and "cur" in parts:
                            split_probs(t, m - 2)
                        if "cur" in parts:
                            exponentials(t, m)
                        for pair, part in heads_split(m):
                            if part in parts:
                                split_heads(t, pair, parts)
                        tile = (t, m + HALF) if m < HALF else (t + 1, m - HALF)
                        if ("cur" if m < HALF else "nxt") in parts:
                            act.wait_ge(ph.qk_full, tile[0] * PAIRS + tile[1] + 1)
                            nc.scalar.copy(qk_hi[:, tile[1], :, :], f0_ps[:].rearrange("p (a s) -> p a s", a=2)).then_inc(ph.qk_hi, 1)
                        if late[1] in parts:
                            f1_unit(t, *late)
                        for unit in xs:
                            if unit[1] in parts:
                                f1_unit(t, *unit)
                over_batches(act, B, iteration)

            act.wait_ge(param_ld, 16 * 10)
            for ph in passes:
                attention(ph)

            def gelu(t, m):
                g = t * FT + m
                act.wait_ge(ff.p_full, g + 1)
                at_least(act, ff.hid_done, g - 1)
                nc.scalar.activation(gate[:, m % 2, :], s_ps[:, m % 4 // 2, m % 2, S:2 * S], ACT.Gelu,
                                     bias=b1_col[:, FT + m:FT + m + 1]).then_inc(ff.gate_done, 1)

            def hidden_hi(t, m):
                act.wait_ge(ff.hid_done, t * FT + m + 1)
                nc.scalar.copy(a_hi[:, m, :], hid[:, m % 2, :]).then_inc(ff.u_hi, 1)

            def iteration(t, parts, parity):
                if parts == FILL:
                    act.wait_ge(ca.f1_done, ca.slots.total)
                    for n in range(8, 11):
                        split_weight(n)
                for m in range(FT):
                    if "cur" in parts:
                        gelu(t, m)
                        if m:
                            hidden_hi(t, m - 1)
                        if m == FT - 1:
                            hidden_hi(t, m)
                    if m == FT - 2 and "nxt" in parts:
                        for k in range(DK):
                            act.wait_ge(ff.x_full, DK * (t + 1) + k + 1)
                            nc.scalar.activation(hT_hi[:, 1 - parity, k, :], pt_ps[:, k, 0:S], ACT.Identity,
                                                 scale=ln_gb[:, 2, 0, k:k + 1],
                                                 bias=ln_gb[:, 2, 1, k:k + 1]).then_inc(ff.x_hi, 1)
            over_batches(act, B, iteration, unroll=2)

        @block.vector
        def _(dve):
            def split_weight(n):
                dve.wait_ge(w_hi_done, n + 1)
                _, scale, slot = staged[n]
                for _, rows, cols in w_pieces(n):
                    op = nc.vector.scalar_tensor_tensor(w_lo[0:rows, slot, cols], w_stage[0:rows, n % 2, cols], scale,
                                                        f32(w_hi[0:rows, slot, cols]), ALU.mult, ALU.subtract)
                op.then_inc(w_done, 1)

            def norm_statistics(ph, b):
                dve.wait_ge(ph.x_ld, 16 * (b + 1))
                for it in range(IT):
                    op = nc.vector.bn_stats(bn[:, it, :], x_ln[:, it, :])
                op.then_inc(ph.bn_done, 1)

            def norm_moments(ph):
                for it in range(IT):
                    op = nc.vector.bn_aggr(mean_var[:, it, :], bn[:, it, :])
                op.then_inc(ph.stats_done, 1)

            def normalise(ph, b):
                dve.wait_ge(ph.rstd_ready, b + 1)
                for it in range(IT):
                    op = nc.vector.tensor_scalar(x_n[:, it, :], x_ln[:, it, :], mean_var[:, it, 0:1], rstd[:, it:it + 1],
                                                 ALU.subtract, ALU.mult)
                op.then_inc(ph.ln_done, 1)

            def attention(ph):
                def maxima(t, m):
                    dve.wait_ge(ph.s_full, t * PAIRS + m + 1)
                    nc.vector.tensor_reduce(neg_max[:, m % 2, :], s_ps[:, m % 2, :, :].rearrange("p h (i j) -> p (h i) j", j=S),
                                            AX_X, ALU.max, negate=True).then_inc(ph.max_done, 1)

                def split_probs(t, m):
                    dve.wait_ge(ph.pt_hi, t * PAIRS + m + 1)
                    nc.vector.tensor_tensor(pT_lo[:, m % 2, :, :], pt_ps[:], f32(pT_hi[:, m % 2, :, :]),
                                            ALU.subtract).then_inc(ph.pt_lo, 1)

                def f1_unit(t, parts, unit, part):
                    b = batch_of(t, part)
                    if unit[0] == "o":
                        g = b * PAIRS + unit[1]
                        dve.wait_ge(ph.o_bot, g + 1)
                        at_least(dve, ph.a_done, g - 1)
                        for hd, part in enumerate((LEFT, RIGHT)):
                            cols = slice(hd * S, (hd + 1) * S)
                            op = nc.vector.tensor_tensor(o_sum[part, unit[1] % 2, :], f1_ps[LEFT, cols], o_lo[:, cols], ALU.add)
                    elif unit[0] == "v":
                        _, c, jt = unit
                        dve.wait_ge(ph.v_hi, 4 * b + 2 * c + jt + 1)
                        heads = slice(c * PAIRS, (c + 1) * PAIRS)
                        op = nc.vector.tensor_tensor(v_hl[:, jt, heads, RIGHT], f1_ps[:].rearrange("p (h d) -> p h d", d=DH),
                                                     f32(v_hl[:, jt, heads, LEFT]), ALU.subtract)
                    elif unit[0] == "x":
                        k = unit[1]
                        dve.wait_ge(ph.x_hi, ph.x_units * b + k + 1)
                        if k < DK:
                            op = nc.vector.tensor_scalar(hT_full[:, 0, k, :], f1_ps[:, 0:S], ln_gb[:, ph.norm, 0, k:k + 1],
                                                         ln_gb[:, ph.norm, 1, k:k + 1], ALU.mult, ALU.add)
                        else:
                            rows = ph.kv_rows[k - DK]
                            op = nc.vector.tensor_copy(hT_full[0:rows, 1, k - DK, :], f1_ps[0:rows, 0:S])
                    else:
                        _, half, it = unit
                        dve.wait_ge(ph.wo_full, 4 * b + 2 * half + it + 1)
                        if half == 0:
                            dve.wait_ge(ph.xrb_done, b + 1)
                            at_least(dve, ph.stored, 16 * b)
                            op = nc.vector.tensor_tensor(x_out[:, it, :], f1_ps[:, 0:D], x_rb[:, it, :], ALU.add)
                        else:
                            dve.wait_ge(ph.f1_done, ph.slots.through(t, ("wo", 0, it), parts))
                            op = nc.vector.tensor_tensor(x_out[:, it, :], f1_ps[:, 0:D], x_out[:, it, :], ALU.add)
                    op.then_inc(ph.f1_done, 1)

                def iteration(t, parts, _parity):
                    for m in range(PAIRS):
                        early, late, *xs = f1_units(m, ph.x_units)
                        if m == 2 and "nxt" in parts:
                            dve.wait_ge(ph.bn_done, t + 2)
                        if "cur" in parts:
                            maxima(t, m)
                        if m == 2 and "nxt" in parts:
                            norm_moments(ph)
                        if early[1] in parts:
                            f1_unit(t, parts, *early)
                        if m < 2 and "prv" in parts:
                            split_probs(t - 1, m + PAIRS - 2)
                        if m >= 2 and "cur" in parts:
                            split_probs(t, m - 2)
                        tile = (t, m + HALF) if m < HALF else (t + 1, m - HALF)
                        if ("cur" if m < HALF else "nxt") in parts:
                            dve.wait_ge(ph.qk_hi, tile[0] * PAIRS + tile[1] + 1)
                            nc.vector.tensor_tensor(qk_lo[:, tile[1], :, :], f0_ps[:].rearrange("p (a s) -> p a s", a=2),
                                                    f32(qk_hi[:, tile[1], :, :]), ALU.subtract).then_inc(ph.qk_lo, 1)
                        if "cur" in parts:
                            dve.wait_ge(ph.exp_done, t * PAIRS + m + 1)
                            nc.vector.reciprocal(row_inv[:, m % 2, :], row_sum[:, m % 2, :]).then_inc(ph.inv_done, 1)
                        if late[1] in parts:
                            f1_unit(t, parts, *late)
                        if m == 1 and "nxt" in parts:
                            norm_statistics(ph, t + 1)
                        if m == 3 and "nxt" in parts:
                            normalise(ph, t + 1)
                            if parts == FILL:
                                for n in range(4):
                                    split_weight(ph.w0 + n)
                        for unit in xs:
                            if unit[1] in parts:
                                f1_unit(t, parts, *unit)
                over_batches(dve, B, iteration)

            dve.wait_ge(param_ld, 16 * 10)
            for ph in passes:
                attention(ph)

            def gated(t, m):
                g = t * FT + m
                dve.wait_ge(ff.gate_done, g + 1)
                at_least(dve, ff.u_lo, g - 1)
                nc.vector.scalar_tensor_tensor(hid[:, m % 2, :], s_ps[:, m % 4 // 2, m % 2, 0:S], b1_col[:, m:m + 1],
                                               gate[:, m % 2, :], ALU.add, ALU.mult).then_inc(ff.hid_done, 1)

            def iteration(t, parts, parity):
                for m in range(FT):
                    if m == 3 and "nxt" in parts:
                        dve.wait_ge(ff.bn_done, t + 2)
                    if "cur" in parts:
                        gated(t, m)
                    if m == 3 and "nxt" in parts:
                        norm_moments(ff)
                    if m == 1 and "prv" in parts:
                        dve.wait_ge(ff.xrb_done, t)
                        at_least(dve, ff.stored, 16 * (t - 1))
                        for it, bank in enumerate((f0_ps, f1_ps)):
                            dve.wait_ge(ff.w2_full, IT * (t - 1) + it + 1)
                            nc.vector.tensor_tensor(x_out[:, it, :], bank[:, 0:D], x_rb[:, it, :], ALU.add).then_inc(ff.y_done, 1)
                    if m == 2 and "nxt" in parts:
                        norm_statistics(ff, t + 1)
                    if m == 4 and "nxt" in parts:
                        normalise(ff, t + 1)
                        if parts == FILL:
                            for n in range(8, 11):
                                split_weight(n)
                    if m == FT - 2 and "nxt" in parts:
                        for k in range(DK):
                            dve.wait_ge(ff.x_hi, DK * (t + 1) + k + 1)
                            nc.vector.tensor_scalar(hT_full[:, 1 - parity, k, :], pt_ps[:, k, 0:S], ln_gb[:, 2, 0, k:k + 1],
                                                    ln_gb[:, 2, 1, k:k + 1], ALU.mult, ALU.add).then_inc(ff.x_mid, 1)
            over_batches(dve, B, iteration, unroll=2)

        @block.gpsimd
        def _(pool):
            nc.gpsimd.memset(neg_half[:], -0.5).then_inc(const_ready, 1)
            nc.gpsimd.memset(eps[:], EPS).then_inc(const_ready, 1)
            nc.gpsimd.memset(ctx_in[:, :, DC:], 0.0).then_inc(const_ready, 1)
            nc.gpsimd.memset(ident[:], 0.0).then_inc(ident_zero, 1)
            pool.wait_ge(ident_zero, 1)
            nc.gpsimd.affine_select(out=ident[:], in_=ident[:], compare_op=ALU.not_equal, fill=1.0, base=0,
                                    pattern=[[-1, P]], channel_multiplier=1).then_inc(const_ready, 1)
            pool.wait_ge(const_ready, 4)
            pool.wait_ge(param_ld, 16 * 10)

            def deviation(ph, b):
                pool.wait_ge(ph.stats_done, b + 1)
                nc.gpsimd.tensor_tensor(var_eps[:], mean_var[:, :, 1], eps[:], ALU.add).then_inc(ph.eps_done, 1)
                pool.wait_ge(ph.eps_done, b + 1)
                nc.gpsimd.tensor_tensor(rstd[:], var_eps[:], neg_half[:], ALU.pow).then_inc(ph.rstd_ready, 1)

            def residual(ph, b, bias):
                pool.wait_ge(ph.res_ld, 16 * (b + 1))
                nc.gpsimd.tensor_tensor(x_rb[:], x_res[:], out_bias[:, bias:bias + 1, :].broadcast_to([P, IT, D]),
                                        ALU.add).then_inc(ph.xrb_done, 1)

            def attention(ph):
                def split_heads(t, m, part):
                    g = batch_of(t, part) * PAIRS + m
                    pool.wait_ge(ph.a_hi_done, g + 1)
                    nc.gpsimd.tensor_tensor(a_lo[:, m, :], o_sum[:, m % 2, :], f32(a_hi[:, m, :]), ALU.subtract).then_inc(ph.a_done, 1)

                def input_lo(t, parts, unit):
                    pool.wait_ge(ph.f1_done, ph.slots.through(t, unit, parts))
                    k = unit[1]
                    side, k, rows = (0, k, P) if k < DK else (1, k - DK, ph.kv_rows[k - DK])
                    nc.gpsimd.tensor_tensor(hT_lo[0:rows, side, k, :], hT_full[0:rows, side, k, :],
                                            f32(hT_hi[0:rows, side, k, :]), ALU.subtract).then_inc(ph.x_lo, 1)

                def iteration(t, parts, _parity):
                    for m in range(PAIRS):
                        early, late, *xs = f1_units(m, ph.x_units)
                        if "cur" in parts:
                            pool.wait_ge(ph.inv_done, t * PAIRS + m + 1)
                            nc.gpsimd.tensor_tensor(probs[:, m % 2, :, :], probs[:, m % 2, :, :],
                                                    row_inv[:, m % 2, :].unsqueeze(2).broadcast_to([P, 2 * IT, S]),
                                                    ALU.mult).then_inc(ph.norm_done, 1)
                        for pair, part in heads_split(m):
                            if part in parts:
                                split_heads(t, pair, part)
                        if m == 2 and "nxt" in parts:
                            deviation(ph, t + 1)
                        if m == 5 and "cur" in parts:
                            if "prv" in parts:
                                pool.wait_ge(ph.f1_done, ph.slots.through(t, ("wo", 0, 1), parts))
                            residual(ph, t, ph.norm)
                        for unit, part in xs:
                            if part in parts:
                                input_lo(t, parts, unit)
                over_batches(pool, B, iteration)

            for ph in passes:
                attention(ph)

            def hidden_lo(t, m):
                pool.wait_ge(ff.u_hi, t * FT + m + 1)
                nc.gpsimd.tensor_tensor(a_lo[:, m, :], hid[:, m % 2, :], f32(a_hi[:, m, :]), ALU.subtract).then_inc(ff.u_lo, 1)

            def iteration(t, parts, parity):
                for m in range(FT):
                    if "cur" in parts:
                        hidden_lo(t, m)
                    if m == 2 and "cur" in parts:
                        at_least(pool, ff.y_done, IT * t)
                        residual(ff, t, 2)
                    if m == 3 and "nxt" in parts:
                        deviation(ff, t + 1)
                    if m == FT - 2 and "nxt" in parts:
                        for k in range(DK):
                            pool.wait_ge(ff.x_mid, DK * (t + 1) + k + 1)
                            nc.gpsimd.tensor_tensor(hT_lo[:, 1 - parity, k, :], hT_full[:, 1 - parity, k, :],
                                                    f32(hT_hi[:, 1 - parity, k, :]), ALU.subtract).then_inc(ff.x_lo, 1)
            over_batches(pool, B, iteration, unroll=2)


_INS = ["x", "ctx_768"] + ["L0_xattn_" + n for n in (
    "ln1_g ln1_b ln2_g ln2_b ln3_g ln3_b sa_wq sa_wk sa_wv sa_wo sa_bo ca_wq ca_wk ca_wv ca_wo ca_bo "
    "ff_w1 ff_b1 ff_w2 ff_b2").split()]


def kernel(**inputs):
    import numpy as _np
    import concourse.bacc as _bacc
    from concourse import mybir as _mybir
    from concourse.bass_utils import run_bass_kernel_spmd as _run

    nc = _bacc.Bacc("TRN2", target_bir_lowering=False, num_devices=1)
    arrays, args = {}, []
    for name in _INS:
        a = _np.ascontiguousarray(inputs[name])
        arrays[f"in_{name}_dram"] = a
        args.append(nc.dram_tensor(f"in_{name}_dram", a.shape, _mybir.dt.from_np(a.dtype), kind="ExternalInput").ap())
    shape = arrays["in_x_dram"].shape
    args.append(nc.dram_tensor("out_dram", shape, F32, kind="ExternalOutput").ap())
    block_kernel(nc, *args)
    r = _run(nc, [arrays], core_ids=[0])
    return r.results[0]["out_dram"]
```

```python
from contextlib import ExitStack

import concourse.bass as bass
from concourse import mybir

F32 = mybir.dt.float32
F32R = mybir.dt.float32r
ALU = mybir.AluOpType
ACT = mybir.ActivationFunctionType
AX_X = mybir.AxisListType.X

P = 128
D = 256
DK = D // P
S = 256
IT = S // P
H = 16
DH = 64
DA = H * DH
PAIRS = H // 2
HALF = PAIRS // 2
EPS = 1e-5
SCALE = DH ** -0.5
DFF = 4 * D
FT = DFF // P
WCOLS = 2048
FILL, START, STEADY, LAST, DRAIN = ("nxt",), ("cur", "nxt"), ("prv", "cur", "nxt"), ("prv", "cur"), ("prv",)
LEFT, RIGHT = slice(0, DH), slice(DH, 2 * DH)


class Units:

    def __init__(self, x_units, batches):
        self.order = [unit for m in range(PAIRS) for unit in units_of(m, x_units)]
        self.batches = batches
        self.before_loop = self._size(FILL) + self._size(START)
        self.total = self.before_loop + (batches - 2) * len(self.order) + self._size(LAST) + self._size(DRAIN)
        assert len(self.order) % 2 == 0

    def _size(self, parts):
        return sum(part in parts for _, part in self.order)

    def _ahead(self, t, parts):
        if parts in (FILL, START):
            return self._size(FILL) if parts == START else 0
        if parts == DRAIN:
            return self.total - self._size(DRAIN)
        return self.before_loop

    def _place(self, unit, parts):
        return [u for u, part in self.order if part in parts].index(unit)

    def through(self, t, unit, parts):
        n = self._ahead(t, parts) + self._place(unit, parts) + 1
        return (t - 1) * len(self.order) + n if parts in (STEADY, LAST) else n

    def ahead(self, t, parts):
        n = self._ahead(t, parts)
        return (t - 1) * len(self.order) + n if parts in (STEADY, LAST) else n

    def bank(self, unit, parts):
        return (self._ahead(None, parts) + self._place(unit, parts)) % 2


def units_of(m, x_units):
    early = [(("wo", 0, 0), "prv"), (("wo", 0, 1), "prv"), (("o", 7), "prv"), (("v", 1, 1), "cur"),
             (("wo", 1, 0), "prv"), (("wo", 1, 1), "prv"), (("o", 3), "cur"), (("v", 0, 1), "nxt")][m]
    qk = (("qk", m + HALF), "cur") if m < HALF else (("qk", m - HALF), "nxt")
    late = [(("o", 5), "prv"), (("o", 6), "prv"), (("v", 1, 0), "cur"), (("o", 0), "cur"),
            (("o", 1), "cur"), (("o", 2), "cur"), (("v", 0, 0), "nxt"), (("o", 4), "cur")][m]
    return [early, qk, late] + ([(("x", k), "nxt") for k in range(x_units)] if m == 3 else [])


def heads_split(m):
    return [[(4, "prv")], [(5, "prv")], [(6, "prv"), (7, "prv")], [], [(0, "cur")], [(1, "cur")], [(2, "cur"), (3, "cur")], []][m]


def pair_behind(t, m, lag, parts):
    if m >= lag:
        return (t, m - lag) if "cur" in parts else None
    return (t - 1, m - lag + PAIRS) if "prv" in parts else None


def batch_of(t, part):
    return t - 1 if part == "prv" else t if part == "cur" else t + 1


def at_least(eng, sem, value):
    if not (isinstance(value, int) and value <= 0):
        eng.wait_ge(sem, value)


def over_batches(eng, batches, iteration, unroll=1):
    iteration(-1, FILL, 1)
    iteration(0, START, 0)
    with eng.Fori(1, batches - unroll, unroll) as t:
        for i in range(unroll):
            iteration(t + i if i else t, STEADY, (1 + i) % 2)
    iteration(batches - 1, LAST, 1)
    iteration(batches, DRAIN, 0)


def block_kernel(nc, x, ctx, ln1_g, ln1_b, ln2_g, ln2_b, ln3_g, ln3_b, sa_wq, sa_wk, sa_wv, sa_wo, sa_bo,
                 ca_wq, ca_wk, ca_wv, ca_wo, ca_bo, ff_w1, ff_b1, ff_w2, ff_b2, out):
    B = x.shape[0]
    DC = ctx.shape[2]
    stack = ExitStack()
    with stack:
        def sb(name, shape, dt=F32):
            return stack.enter_context(nc.sbuf_tensor(name, shape, dt))

        def psum(name, shape):
            return stack.enter_context(nc.psum_tensor(name, shape, F32))

        def sem(name):
            return stack.enter_context(nc.semaphore(name))

        x_sa = nc.dram_tensor("x_sa_dram", (B, S, D), F32).ap()
        x_ca = nc.dram_tensor("x_ca_dram", (B, S, D), F32).ap()

        s_ps = psum("s_ps", [P, 2, 2, IT * S])
        pt_ps = psum("pt_ps", [P, 2, 2 * S])
        unit_ps = psum("unit_ps", [P, 2, 2 * S])

        w_hi = sb("w_hi", [P, 4, WCOLS], F32R)
        w_lo = sb("w_lo", [P, 4, WCOLS], F32R)
        w_stage = sb("w_stage", [P, 2, WCOLS])
        ln_gb = sb("ln_gb", [P, 3, 2, DK])
        b1_col = sb("b1_col", [P, 2 * FT])
        out_bias = sb("out_bias", [P, 3, D])
        ident = sb("ident", [P, P])
        neg_half = sb("neg_half", [P, IT])
        eps = sb("eps", [P, IT])

        x_ln = sb("x_ln", [P, IT, D])
        x_n = sb("x_n", [P, IT, D])
        ctx_in = sb("ctx_in", [P, IT, DK * P])
        x_res = sb("x_res", [P, IT, D])
        x_rb = sb("x_rb", [P, IT, D])
        x_out = sb("x_out", [P, IT, D])
        bn = sb("bn", [P, IT, 6])
        mean_var = sb("mean_var", [P, IT, 2])
        var_eps = sb("var_eps", [P, IT])
        rstd = sb("rstd", [P, IT])
        hT_full = sb("hT_full", [P, 2, DK, S])
        hT_hi = sb("hT_hi", [P, 2, DK, S], F32R)
        hT_lo = sb("hT_lo", [P, 2, DK, S], F32R)
        qk_hi = sb("qk_hi", [P, PAIRS, 2, S], F32R)
        qk_lo = sb("qk_lo", [P, PAIRS, 2, S], F32R)
        v_hl = sb("v_hl", [P, IT, H, 2 * DH], F32R)
        probs = sb("probs", [P, 2, 2 * IT, S])
        neg_max = sb("neg_max", [P, 2, 2 * IT])
        row_sum = sb("row_sum", [P, 2, 2 * IT])
        row_inv = sb("row_inv", [P, 2, 2 * IT])
        pT_hi = sb("pT_hi", [P, 2, 2, 2 * S], F32R)
        pT_lo = sb("pT_lo", [P, 2, 2, 2 * S], F32R)
        o_lo = sb("o_lo", [DH, 2, 2 * S])
        o_sum = sb("o_sum", [P, 2, S])
        a_hi = sb("a_hi", [P, PAIRS, S], F32R)
        a_lo = sb("a_lo", [P, PAIRS, S], F32R)
        gate = sb("gate", [P, 2, S])
        hid = sb("hid", [P, 2, S])

        const_ready = sem("const_ready")
        ident_zero = sem("ident_zero")
        param_ld = sem("param_ld")
        stage_ld = [sem("stage_ld0"), sem("stage_ld1")]
        w_hi_done = sem("w_hi_done")
        w_done = sem("w_done")

        class NormSemaphores:

            def __init__(self, name):
                self.x_ld = sem(f"{name}_x_ld")
                self.res_ld = sem(f"{name}_res_ld")
                self.stored = sem(f"{name}_stored")
                self.bn_done = sem(f"{name}_bn_done")
                self.stats_done = sem(f"{name}_stats_done")
                self.eps_done = sem(f"{name}_eps_done")
                self.rstd_ready = sem(f"{name}_rstd_ready")
                self.ln_done = sem(f"{name}_ln_done")
                self.x_full = sem(f"{name}_x_full")
                self.x_hi = sem(f"{name}_x_hi")
                self.x_lo = sem(f"{name}_x_lo")
                self.xrb_done = sem(f"{name}_xrb_done")

        class AttentionPass(NormSemaphores):

            def __init__(self, name, norm, x_in, x_to, ctx_rows, weights, w0, before):
                super().__init__(name)
                self.norm, self.x_in, self.x_to, self.weights, self.w0, self.before = norm, x_in, x_to, weights, w0, before
                self.kv = 1 if ctx_rows else 0
                self.kv_rows = ctx_rows or [P] * DK
                self.x_units = DK * (2 if ctx_rows else 1)
                self.units = Units(self.x_units, B)
                self.ctx_ld = sem(f"{name}_ctx_ld")
                self.qk_full = sem(f"{name}_qk_full")
                self.qk_hi = sem(f"{name}_qk_hi")
                self.v_full = sem(f"{name}_v_full")
                self.v_hi = sem(f"{name}_v_hi")
                self.s_full = sem(f"{name}_s_full")
                self.max_done = sem(f"{name}_max_done")
                self.exp_done = sem(f"{name}_exp_done")
                self.inv_done = sem(f"{name}_inv_done")
                self.norm_done = sem(f"{name}_norm_done")
                self.pt_full = sem(f"{name}_pt_full")
                self.pt_hi = sem(f"{name}_pt_hi")
                self.pt_lo = sem(f"{name}_pt_lo")
                self.o_full = sem(f"{name}_o_full")
                self.o_bot = sem(f"{name}_o_bot")
                self.a_hi_done = sem(f"{name}_a_hi_done")
                self.a_done = sem(f"{name}_a_done")
                self.wo_full = sem(f"{name}_wo_full")
                self.unit_done = sem(f"{name}_unit_done")

        class FeedForwardPass(NormSemaphores):
            def __init__(self, name):
                super().__init__(name)
                self.x_mid = sem(f"{name}_x_mid")
                self.p_full = sem(f"{name}_p_full")
                self.gate_done = sem(f"{name}_gate_done")
                self.hid_done = sem(f"{name}_hid_done")
                self.u_hi = sem(f"{name}_u_hi")
                self.u_lo = sem(f"{name}_u_lo")
                self.w2_full = sem(f"{name}_w2_full")
                self.y_done = sem(f"{name}_y_done")

        sa = AttentionPass("sa", 0, x, x_sa, None, [(sa_wq, SCALE), (sa_wk, 1.0), (sa_wv, 1.0), (sa_wo, 1.0)], 0, None)
        ca = AttentionPass("ca", 1, x_sa, x_ca, [P, DC - P], [(ca_wq, SCALE), (ca_wk, 1.0), (ca_wv, 1.0), (ca_wo, 1.0)], 4, sa)
        ff = FeedForwardPass("ff")
        passes = (sa, ca)

        w1_v = ff_w1.rearrange("(k p) n -> p k n", p=P)
        staged = [(w, scale, slot) for ph in passes for slot, (w, scale) in enumerate(ph.weights)]
        staged += [(w1_v[:, 0, :], 1.0, 0), (w1_v[:, 1, :], 1.0, 1), (ff_w2, 1.0, 2)]

        def w_pieces(n):
            w = staged[n][0]
            if w.shape[0] == P:
                return [(w, P, slice(0, WCOLS))]
            if w.shape[0] % P:
                cols = w.shape[1]
                return [(w[0:P, :], P, slice(0, cols)), (w[P:, :], w.shape[0] - P, slice(cols, 2 * cols))]
            return [(w.rearrange("(k p) n -> p k n", p=P), P, slice(0, WCOLS))]

        def tiles(a):
            return a.rearrange("(i p) d -> p i d", p=P)

        def f32(a):
            return a.bitcast(F32)

        block = stack.enter_context(nc.Block())

        @block.sync
        def _(sp):
            def load_weight(n):
                if n >= 2:
                    sp.wait_ge(w_done, n - 1)
                for w, rows, cols in w_pieces(n):
                    dst = w_stage[0:rows, n % 2, cols]
                    if len(w.shape) == 3:
                        dst = dst.rearrange("p (k n) -> p k n", k=w.shape[1])
                    sp.dma_start(dst, w).then_inc(stage_ld[n % 2], 16)

            def attention(ph):
                def iteration(t, parts, _parity):
                    if "nxt" in parts:
                        at_least(sp, ph.ln_done, t + 1)
                        sp.dma_start(x_ln[:], tiles(ph.x_in[t + 1])).then_inc(ph.x_ld, 16)
                        if ph.kv:
                            at_least(sp, ph.x_full, ph.x_units * (t + 1))
                            sp.dma_start(ctx_in[:, :, 0:DC], tiles(ctx[t + 1])).then_inc(ph.ctx_ld, 16)
                    if parts == FILL:
                        for n in range(4):
                            load_weight(ph.w0 + n)
                    if "prv" in parts:
                        sp.wait_ge(ph.unit_done, ph.units.through(t, ("wo", 1, 1), parts))
                        sp.dma_start(tiles(ph.x_to[t - 1]), x_out[:]).then_inc(ph.stored, 16)
                        sp.wait_ge(ph.stored, 16 * t)
                    if "cur" in parts:
                        at_least(sp, ph.xrb_done, t)
                        sp.dma_start(x_res[:], tiles(ph.x_in[t])).then_inc(ph.res_ld, 16)
                over_batches(sp, B, iteration)
                sp.wait_ge(ph.stored, 16 * B)

            for i, (g, b) in enumerate(((ln1_g, ln1_b), (ln2_g, ln2_b), (ln3_g, ln3_b))):
                sp.dma_start(ln_gb[:, i, 0, :], g.rearrange("(k p) -> p k", p=P),
                             allow_slow_non_contiguous=True).then_inc(param_ld, 16)
                sp.dma_start(ln_gb[:, i, 1, :], b.rearrange("(k p) -> p k", p=P),
                             allow_slow_non_contiguous=True).then_inc(param_ld, 16)
            sp.dma_start(b1_col[:], ff_b1.rearrange("(k p) -> p k", p=P),
                             allow_slow_non_contiguous=True).then_inc(param_ld, 16)
            for i, b in enumerate((sa_bo, ca_bo, ff_b2)):
                sp.dma_start(out_bias[:, i, :], b.unsqueeze(0).broadcast_to([P, D])).then_inc(param_ld, 16)
            for ph in passes:
                attention(ph)

            def iteration(t, parts, _parity):
                if "nxt" in parts:
                    at_least(sp, ff.ln_done, t + 1)
                    sp.dma_start(x_ln[:], tiles(x_ca[t + 1])).then_inc(ff.x_ld, 16)
                if parts == FILL:
                    for n in range(8, 11):
                        load_weight(n)
                if "prv" in parts:
                    sp.wait_ge(ff.y_done, IT * t)
                    sp.dma_start(tiles(out[t - 1]), x_out[:]).then_inc(ff.stored, 16)
                    sp.wait_ge(ff.stored, 16 * t)
                if "cur" in parts:
                    at_least(sp, ff.xrb_done, t)
                    sp.dma_start(x_res[:], tiles(x_ca[t])).then_inc(ff.res_ld, 16)
            over_batches(sp, B, iteration, unroll=2)
            sp.wait_ge(ff.stored, 16 * B)

        @block.tensor
        def _(pe):
            def product(dst, pairs, start=True, stop=True):
                terms = [(a, b) for a_hi_, a_lo_, b_hi_, b_lo_ in pairs
                         for a, b in ((a_hi_, b_hi_), (a_hi_, b_lo_), (a_lo_, b_hi_))]
                for n, (a, b) in enumerate(terms):
                    last = nc.tensor.matmul(dst, a, b, start=start and n == 0, stop=stop and n == len(terms) - 1)
                return last

            def attention(ph):
                def scores(t, m):
                    g = t * PAIRS + m
                    at_least(pe, ph.exp_done, g - 1)
                    for it in range(IT):
                        rows = slice(it * P, (it + 1) * P)
                        for n, (q, k) in enumerate(((qk_hi, qk_hi), (qk_hi, qk_lo), (qk_lo, qk_hi))):
                            for hd, part in enumerate((LEFT, RIGHT)):
                                last = nc.tensor.matmul(s_ps[:, m % 2, hd, it * S:(it + 1) * S], q[part, m, 0, rows],
                                                        k[part, m, 1, :], start=n == 0, stop=n == 2)
                    last.then_inc(ph.s_full, 1)

                def transpose_probs(t, m):
                    g = t * PAIRS + m
                    pe.wait_ge(ph.norm_done, g + 1)
                    at_least(pe, ph.pt_lo, g)
                    for hd in range(2):
                        for jt in range(IT):
                            for it in range(IT):
                                last = nc.tensor.transpose(pt_ps[:, hd, jt * S + it * P:jt * S + (it + 1) * P],
                                                           probs[:, m % 2, hd * IT + it, jt * P:(jt + 1) * P], ident[:])
                    last.then_inc(ph.pt_full, 1)

                def run_unit(t, parts, unit, part):
                    b = batch_of(t, part)
                    bank = unit_ps[:, ph.units.bank(unit, parts), :]
                    at_least(pe, ph.unit_done, ph.units.through(t, unit, parts) - 2)
                    if unit[0] == "qk":
                        m = unit[1]
                        if parts == FILL and m == 0:
                            pe.wait_ge(w_done, ph.w0 + 2)
                        pe.wait_ge(ph.x_lo, ph.x_units * (b + 1))
                        cols = [slice(k * DA + m * P, k * DA + (m + 1) * P) for k in range(DK)]
                        product(bank[:, 0:S], [(w_hi[:, 0, cols[k]], w_lo[:, 0, cols[k]], hT_hi[:, 0, k, :], hT_lo[:, 0, k, :])
                                               for k in range(DK)])
                        product(bank[:, S:2 * S],
                                [(w_hi[0:r, 1, cols[k]], w_lo[0:r, 1, cols[k]], hT_hi[0:r, ph.kv, k, :], hT_lo[0:r, ph.kv, k, :])
                                 for k, r in enumerate(ph.kv_rows)]).then_inc(ph.qk_full, 1)
                    elif unit[0] == "wo":
                        _, half, it = unit
                        pe.wait_ge(ph.a_done, b * PAIRS + (half + 1) * HALF)
                        rows = slice(it * P, (it + 1) * P)
                        product(bank[:, 0:D],
                                [(a_hi[:, m, rows], a_lo[:, m, rows], w_hi[:, 3, m * D:(m + 1) * D], w_lo[:, 3, m * D:(m + 1) * D])
                                 for m in range(half * HALF, (half + 1) * HALF)]).then_inc(ph.wo_full, 1)
                    elif unit[0] == "o":
                        m = unit[1]
                        pe.wait_ge(ph.pt_lo, b * PAIRS + m + 1)
                        for hd in range(2):
                            for n, (jt, pT) in enumerate((jt, pT) for jt in range(IT) for pT in (pT_hi, pT_lo)):
                                last = nc.tensor.matmul(bank[:, hd * S:(hd + 1) * S], v_hl[:, jt, 2 * m + hd, :],
                                                        pT[:, m % 2, hd, jt * S:(jt + 1) * S], start=n == 0, stop=n == 3)
                        last.then_inc(ph.o_full, 1)
                    elif unit[0] == "v":
                        _, c, jt = unit
                        if parts == FILL and jt == 0:
                            pe.wait_ge(w_done, ph.w0 + 3)
                        rows = slice(jt * P, (jt + 1) * P)
                        cols = [slice(k * DA + c * 2 * S, k * DA + (c + 1) * 2 * S) for k in range(DK)]
                        product(bank,
                                [(hT_hi[0:r, ph.kv, k, rows], hT_lo[0:r, ph.kv, k, rows], w_hi[0:r, 2, cols[k]], w_lo[0:r, 2, cols[k]])
                                 for k, r in enumerate(ph.kv_rows)]).then_inc(ph.v_full, 1)
                    else:
                        k = unit[1]
                        if k == 0:
                            pe.wait_ge(ph.ln_done, b + 1)
                        elif k == DK:
                            pe.wait_ge(ph.ctx_ld, 16 * (b + 1))
                        src, k = (x_n, k) if k < DK else (ctx_in, k - DK)
                        for it in range(IT):
                            last = nc.tensor.transpose(bank[:, it * P:(it + 1) * P], src[:, it, k * P:(k + 1) * P], ident[:])
                        last.then_inc(ph.x_full, 1)

                def iteration(t, parts, _parity):
                    if parts == START:
                        pe.wait_ge(w_done, ph.w0 + 4)
                    for m in range(PAIRS):
                        early, qk, *late = units_of(m, ph.x_units)
                        if early[1] in parts:
                            run_unit(t, parts, *early)
                        if "cur" in parts:
                            scores(t, m)
                        if qk[1] in parts:
                            run_unit(t, parts, *qk)
                        if behind := pair_behind(t, m, 2, parts):
                            transpose_probs(*behind)
                        for unit in late:
                            if unit[1] in parts:
                                run_unit(t, parts, *unit)
                over_batches(pe, B, iteration)

            pe.wait_ge(const_ready, 4)
            for ph in passes:
                attention(ph)

            def hidden(t, m, parity):
                g = t * FT + m
                if m == 0:
                    pe.wait_ge(ff.x_lo, DK * (t + 1))
                at_least(pe, ff.hid_done, g - 3)
                for half in range(2):
                    cols = slice(half * DFF + m * P, half * DFF + (m + 1) * P)
                    last = product(s_ps[:, m % 4 // 2, m % 2, half * S:(half + 1) * S],
                                   [(w_hi[:, k, cols], w_lo[:, k, cols], hT_hi[:, parity, k, :], hT_lo[:, parity, k, :])
                                    for k in range(DK)])
                last.then_inc(ff.p_full, 1)

            def down(b, m):
                pe.wait_ge(ff.u_lo, b * FT + m + 1)
                if m == 0:
                    at_least(pe, ff.y_done, IT * b)
                for it, bank in enumerate((unit_ps[:, 0, :], unit_ps[:, 1, :])):
                    rows = slice(it * P, (it + 1) * P)
                    last = product(bank[:, 0:D], [(a_hi[:, m, rows], a_lo[:, m, rows],
                                                   w_hi[:, 2, m * D:(m + 1) * D], w_lo[:, 2, m * D:(m + 1) * D])],
                                   start=m == 0, stop=m == FT - 1)
                    if m == FT - 1:
                        last.then_inc(ff.w2_full, 1)

            def iteration(t, parts, parity):
                if parts == START:
                    pe.wait_ge(w_done, len(staged))
                for m in range(FT):
                    if "cur" in parts:
                        hidden(t, m, parity)
                    if m < 2 and "prv" in parts:
                        down(t - 1, m + FT - 2)
                    if m >= 2 and "cur" in parts:
                        down(t, m - 2)
                    if m == FT - 2 and "nxt" in parts:
                        pe.wait_ge(ff.ln_done, t + 2)
                        for k in range(DK):
                            at_least(pe, ff.x_mid, DK * (t + 1) + k - 1)
                            for it in range(IT):
                                last = nc.tensor.transpose(pt_ps[:, k, it * P:(it + 1) * P],
                                                           x_n[:, it, k * P:(k + 1) * P], ident[:])
                            last.then_inc(ff.x_full, 1)
            over_batches(pe, B, iteration, unroll=2)

        @block.scalar
        def _(act):
            def split_weight(n):
                pieces = w_pieces(n)
                act.wait_ge(stage_ld[n % 2], 16 * sum(len(w_pieces(k)) for k in range(n % 2, n + 1, 2)))
                _, scale, slot = staged[n]
                for i, (_, rows, cols) in enumerate(pieces):
                    op = nc.scalar.activation(w_hi[0:rows, slot, cols], w_stage[0:rows, n % 2, cols], ACT.Copy, scale=scale)
                op.then_inc(w_hi_done, 1)

            def attention(ph):
                def split_probs(t, m):
                    act.wait_ge(ph.pt_full, t * PAIRS + m + 1)
                    nc.scalar.copy(pT_hi[:, m % 2, :, :], pt_ps[:]).then_inc(ph.pt_hi, 1)

                def split_heads(t, m, parts):
                    done = ph.units.ahead(t, parts) if m == HALF else ph.units.through(t, ("o", m), parts)
                    act.wait_ge(ph.unit_done, done)
                    nc.scalar.copy(a_hi[:, m, :], o_sum[:, m % 2, :]).then_inc(ph.a_hi_done, 1)

                def exponentials(t, m):
                    act.wait_ge(ph.max_done, t * PAIRS + m + 1)
                    for r in range(2 * IT):
                        op = nc.scalar.activation(probs[:, m % 2, r, :], s_ps[:, m % 2, r // IT, r % IT * S:(r % IT + 1) * S],
                                                  ACT.Exp, bias=neg_max[:, m % 2, r:r + 1],
                                                  accum_out=row_sum[:, m % 2, r:r + 1])
                    op.then_inc(ph.exp_done, 1)

                def split_unit(t, parts, unit, part):
                    b = batch_of(t, part)
                    bank = unit_ps[:, ph.units.bank(unit, parts), :]
                    if unit[0] == "qk":
                        act.wait_ge(ph.qk_full, b * PAIRS + unit[1] + 1)
                        nc.scalar.copy(qk_hi[:, unit[1], :, :], bank.rearrange("p (a s) -> p a s", a=2)).then_inc(ph.qk_hi, 1)
                    elif unit[0] == "o":
                        act.wait_ge(ph.o_full, b * PAIRS + unit[1] + 1)
                        nc.scalar.copy(o_lo[:, unit[1] % 2, :], bank[DH:P, :]).then_inc(ph.o_bot, 1)
                    elif unit[0] == "v":
                        _, c, jt = unit
                        act.wait_ge(ph.v_full, 4 * b + 2 * c + jt + 1)
                        nc.scalar.copy(v_hl[:, jt, c * PAIRS:(c + 1) * PAIRS, LEFT],
                                       bank.rearrange("p (h d) -> p h d", d=DH)).then_inc(ph.v_hi, 1)
                    elif unit[0] == "x":
                        k = unit[1]
                        act.wait_ge(ph.x_full, ph.x_units * b + k + 1)
                        if k < DK:
                            nc.scalar.activation(hT_hi[:, 0, k, :], bank[:, 0:S], ACT.Identity,
                                                 scale=ln_gb[:, ph.norm, 0, k:k + 1],
                                                 bias=ln_gb[:, ph.norm, 1, k:k + 1]).then_inc(ph.x_hi, 1)
                        else:
                            rows = ph.kv_rows[k - DK]
                            nc.scalar.copy(hT_hi[0:rows, 1, k - DK, :], bank[0:rows, 0:S]).then_inc(ph.x_hi, 1)

                def iteration(t, parts, _parity):
                    if parts == FILL:
                        if ph.before:
                            act.wait_ge(ph.before.unit_done, ph.before.units.total)
                        for n in range(4):
                            split_weight(ph.w0 + n)
                    for m in range(PAIRS):
                        early, qk, *late = units_of(m, ph.x_units)
                        if behind := pair_behind(t, m, 1, parts):
                            exponentials(*behind)
                        if early[1] in parts:
                            split_unit(t, parts, *early)
                        for pair, part in heads_split(m):
                            if part in parts:
                                split_heads(t, pair, parts)
                        if qk[1] in parts:
                            split_unit(t, parts, *qk)
                        if behind := pair_behind(t, m, 2, parts):
                            split_probs(*behind)
                        for unit in late:
                            if unit[1] in parts:
                                split_unit(t, parts, *unit)
                over_batches(act, B, iteration)

            act.wait_ge(param_ld, 16 * 10)
            for ph in passes:
                attention(ph)

            def gelu(t, m):
                g = t * FT + m
                act.wait_ge(ff.p_full, g + 1)
                at_least(act, ff.hid_done, g - 1)
                nc.scalar.activation(gate[:, m % 2, :], s_ps[:, m % 4 // 2, m % 2, S:2 * S], ACT.Gelu,
                                     bias=b1_col[:, FT + m:FT + m + 1]).then_inc(ff.gate_done, 1)

            def hidden_hi(t, m):
                act.wait_ge(ff.hid_done, t * FT + m + 1)
                nc.scalar.copy(a_hi[:, m, :], hid[:, m % 2, :]).then_inc(ff.u_hi, 1)

            def iteration(t, parts, parity):
                if parts == FILL:
                    act.wait_ge(ca.unit_done, ca.units.total)
                    for n in range(8, 11):
                        split_weight(n)
                for m in range(FT):
                    if "cur" in parts:
                        gelu(t, m)
                        if m:
                            hidden_hi(t, m - 1)
                        if m == FT - 1:
                            hidden_hi(t, m)
                    if m == FT - 2 and "nxt" in parts:
                        for k in range(DK):
                            act.wait_ge(ff.x_full, DK * (t + 1) + k + 1)
                            nc.scalar.activation(hT_hi[:, 1 - parity, k, :], pt_ps[:, k, 0:S], ACT.Identity,
                                                 scale=ln_gb[:, 2, 0, k:k + 1],
                                                 bias=ln_gb[:, 2, 1, k:k + 1]).then_inc(ff.x_hi, 1)
            over_batches(act, B, iteration, unroll=2)

        @block.vector
        def _(dve):
            def split_weight(n):
                dve.wait_ge(w_hi_done, n + 1)
                _, scale, slot = staged[n]
                for _, rows, cols in w_pieces(n):
                    op = nc.vector.scalar_tensor_tensor(w_lo[0:rows, slot, cols], w_stage[0:rows, n % 2, cols], scale,
                                                        f32(w_hi[0:rows, slot, cols]), ALU.mult, ALU.subtract)
                op.then_inc(w_done, 1)

            def norm_statistics(ph, b):
                dve.wait_ge(ph.x_ld, 16 * (b + 1))
                for it in range(IT):
                    op = nc.vector.bn_stats(bn[:, it, :], x_ln[:, it, :])
                op.then_inc(ph.bn_done, 1)

            def norm_moments(ph):
                for it in range(IT):
                    op = nc.vector.bn_aggr(mean_var[:, it, :], bn[:, it, :])
                op.then_inc(ph.stats_done, 1)

            def normalise(ph, b):
                dve.wait_ge(ph.rstd_ready, b + 1)
                for it in range(IT):
                    op = nc.vector.tensor_scalar(x_n[:, it, :], x_ln[:, it, :], mean_var[:, it, 0:1], rstd[:, it:it + 1],
                                                 ALU.subtract, ALU.mult)
                op.then_inc(ph.ln_done, 1)

            def attention(ph):
                def maxima(t, m):
                    dve.wait_ge(ph.s_full, t * PAIRS + m + 1)
                    nc.vector.tensor_reduce(neg_max[:, m % 2, :], s_ps[:, m % 2, :, :].rearrange("p h (i j) -> p (h i) j", j=S),
                                            AX_X, ALU.max, negate=True).then_inc(ph.max_done, 1)

                def invert_sums(t, m):
                    dve.wait_ge(ph.exp_done, t * PAIRS + m + 1)
                    nc.vector.reciprocal(row_inv[:, m % 2, :], row_sum[:, m % 2, :]).then_inc(ph.inv_done, 1)

                def split_probs(t, m):
                    dve.wait_ge(ph.pt_hi, t * PAIRS + m + 1)
                    nc.vector.tensor_tensor(pT_lo[:, m % 2, :, :], pt_ps[:], f32(pT_hi[:, m % 2, :, :]),
                                            ALU.subtract).then_inc(ph.pt_lo, 1)

                def finish_unit(t, parts, unit, part):
                    b = batch_of(t, part)
                    bank = unit_ps[:, ph.units.bank(unit, parts), :]
                    if unit[0] == "qk":
                        m = unit[1]
                        dve.wait_ge(ph.qk_hi, b * PAIRS + m + 1)
                        op = nc.vector.tensor_tensor(qk_lo[:, m, :, :], bank.rearrange("p (a s) -> p a s", a=2),
                                                     f32(qk_hi[:, m, :, :]), ALU.subtract)
                    elif unit[0] == "o":
                        g = b * PAIRS + unit[1]
                        dve.wait_ge(ph.o_bot, g + 1)
                        at_least(dve, ph.a_done, g - 1)
                        for hd, part in enumerate((LEFT, RIGHT)):
                            cols = slice(hd * S, (hd + 1) * S)
                            op = nc.vector.tensor_tensor(o_sum[part, unit[1] % 2, :], bank[LEFT, cols], o_lo[:, unit[1] % 2, cols], ALU.add)
                    elif unit[0] == "v":
                        _, c, jt = unit
                        dve.wait_ge(ph.v_hi, 4 * b + 2 * c + jt + 1)
                        heads = slice(c * PAIRS, (c + 1) * PAIRS)
                        op = nc.vector.tensor_tensor(v_hl[:, jt, heads, RIGHT], bank.rearrange("p (h d) -> p h d", d=DH),
                                                     f32(v_hl[:, jt, heads, LEFT]), ALU.subtract)
                    elif unit[0] == "x":
                        k = unit[1]
                        dve.wait_ge(ph.x_hi, ph.x_units * b + k + 1)
                        if k < DK:
                            op = nc.vector.tensor_scalar(hT_full[:, 0, k, :], bank[:, 0:S], ln_gb[:, ph.norm, 0, k:k + 1],
                                                         ln_gb[:, ph.norm, 1, k:k + 1], ALU.mult, ALU.add)
                        else:
                            rows = ph.kv_rows[k - DK]
                            op = nc.vector.tensor_copy(hT_full[0:rows, 1, k - DK, :], bank[0:rows, 0:S])
                    else:
                        _, half, it = unit
                        dve.wait_ge(ph.wo_full, 4 * b + 2 * half + it + 1)
                        if half == 0:
                            dve.wait_ge(ph.xrb_done, b + 1)
                            op = nc.vector.tensor_tensor(x_out[:, it, :], bank[:, 0:D], x_rb[:, it, :], ALU.add)
                        else:
                            dve.wait_ge(ph.unit_done, ph.units.through(t, ("wo", 0, it), parts))
                            op = nc.vector.tensor_tensor(x_out[:, it, :], bank[:, 0:D], x_out[:, it, :], ALU.add)
                    op.then_inc(ph.unit_done, 1)

                def iteration(t, parts, _parity):
                    for m in range(PAIRS):
                        early, qk, *late = units_of(m, ph.x_units)
                        if early[1] in parts:
                            finish_unit(t, parts, *early)
                        if behind := pair_behind(t, m, 1, parts):
                            invert_sums(*behind)
                        if m == 2 and "nxt" in parts:
                            dve.wait_ge(ph.bn_done, t + 2)
                        if "cur" in parts:
                            maxima(t, m)
                        if m == 2 and "nxt" in parts:
                            norm_moments(ph)
                        if qk[1] in parts:
                            finish_unit(t, parts, *qk)
                        if behind := pair_behind(t, m, 2, parts):
                            split_probs(*behind)
                        if m == 1 and "nxt" in parts:
                            norm_statistics(ph, t + 1)
                        if m == 3 and "nxt" in parts:
                            normalise(ph, t + 1)
                            if parts == FILL:
                                for n in range(4):
                                    split_weight(ph.w0 + n)
                        for unit in late:
                            if unit[1] in parts:
                                finish_unit(t, parts, *unit)
                over_batches(dve, B, iteration)

            dve.wait_ge(param_ld, 16 * 10)
            for ph in passes:
                attention(ph)

            def gated(t, m):
                g = t * FT + m
                dve.wait_ge(ff.gate_done, g + 1)
                at_least(dve, ff.u_lo, g - 1)
                nc.vector.scalar_tensor_tensor(hid[:, m % 2, :], s_ps[:, m % 4 // 2, m % 2, 0:S], b1_col[:, m:m + 1],
                                               gate[:, m % 2, :], ALU.add, ALU.mult).then_inc(ff.hid_done, 1)

            def iteration(t, parts, parity):
                for m in range(FT):
                    if m == 3 and "nxt" in parts:
                        dve.wait_ge(ff.bn_done, t + 2)
                    if "cur" in parts:
                        gated(t, m)
                    if m == 3 and "nxt" in parts:
                        norm_moments(ff)
                    if m == 1 and "prv" in parts:
                        dve.wait_ge(ff.xrb_done, t)
                        for it, bank in enumerate((unit_ps[:, 0, :], unit_ps[:, 1, :])):
                            dve.wait_ge(ff.w2_full, IT * (t - 1) + it + 1)
                            nc.vector.tensor_tensor(x_out[:, it, :], bank[:, 0:D], x_rb[:, it, :], ALU.add).then_inc(ff.y_done, 1)
                    if m == 2 and "nxt" in parts:
                        norm_statistics(ff, t + 1)
                    if m == 4 and "nxt" in parts:
                        normalise(ff, t + 1)
                        if parts == FILL:
                            for n in range(8, 11):
                                split_weight(n)
                    if m == FT - 2 and "nxt" in parts:
                        for k in range(DK):
                            dve.wait_ge(ff.x_hi, DK * (t + 1) + k + 1)
                            nc.vector.tensor_scalar(hT_full[:, 1 - parity, k, :], pt_ps[:, k, 0:S], ln_gb[:, 2, 0, k:k + 1],
                                                    ln_gb[:, 2, 1, k:k + 1], ALU.mult, ALU.add).then_inc(ff.x_mid, 1)
            over_batches(dve, B, iteration, unroll=2)

        @block.gpsimd
        def _(pool):
            nc.gpsimd.memset(neg_half[:], -0.5).then_inc(const_ready, 1)
            nc.gpsimd.memset(eps[:], EPS).then_inc(const_ready, 1)
            nc.gpsimd.memset(ctx_in[:, :, DC:], 0.0).then_inc(const_ready, 1)
            nc.gpsimd.memset(ident[:], 0.0).then_inc(ident_zero, 1)
            pool.wait_ge(ident_zero, 1)
            nc.gpsimd.affine_select(out=ident[:], in_=ident[:], compare_op=ALU.not_equal, fill=1.0, base=0,
                                    pattern=[[-1, P]], channel_multiplier=1).then_inc(const_ready, 1)
            pool.wait_ge(const_ready, 4)
            pool.wait_ge(param_ld, 16 * 10)

            def deviation(ph, b):
                pool.wait_ge(ph.stats_done, b + 1)
                nc.gpsimd.tensor_tensor(var_eps[:], mean_var[:, :, 1], eps[:], ALU.add).then_inc(ph.eps_done, 1)
                pool.wait_ge(ph.eps_done, b + 1)
                nc.gpsimd.tensor_tensor(rstd[:], var_eps[:], neg_half[:], ALU.pow).then_inc(ph.rstd_ready, 1)

            def residual(ph, b, bias):
                pool.wait_ge(ph.res_ld, 16 * (b + 1))
                nc.gpsimd.tensor_tensor(x_rb[:], x_res[:], out_bias[:, bias:bias + 1, :].broadcast_to([P, IT, D]),
                                        ALU.add).then_inc(ph.xrb_done, 1)

            def attention(ph):
                def split_heads(t, m, part):
                    g = batch_of(t, part) * PAIRS + m
                    pool.wait_ge(ph.a_hi_done, g + 1)
                    nc.gpsimd.tensor_tensor(a_lo[:, m, :], o_sum[:, m % 2, :], f32(a_hi[:, m, :]), ALU.subtract).then_inc(ph.a_done, 1)

                def normalise(t, m):
                    pool.wait_ge(ph.inv_done, t * PAIRS + m + 1)
                    nc.gpsimd.tensor_tensor(probs[:, m % 2, :, :], probs[:, m % 2, :, :],
                                            row_inv[:, m % 2, :].unsqueeze(2).broadcast_to([P, 2 * IT, S]),
                                            ALU.mult).then_inc(ph.norm_done, 1)

                def input_lo(t, parts, unit):
                    pool.wait_ge(ph.unit_done, ph.units.through(t, unit, parts))
                    k = unit[1]
                    side, k, rows = (0, k, P) if k < DK else (1, k - DK, ph.kv_rows[k - DK])
                    nc.gpsimd.tensor_tensor(hT_lo[0:rows, side, k, :], hT_full[0:rows, side, k, :],
                                            f32(hT_hi[0:rows, side, k, :]), ALU.subtract).then_inc(ph.x_lo, 1)

                def iteration(t, parts, _parity):
                    for m in range(PAIRS):
                        if behind := pair_behind(t, m, 1, parts):
                            normalise(*behind)
                        for pair, part in heads_split(m):
                            if part in parts:
                                split_heads(t, pair, part)
                        if m == 2 and "nxt" in parts:
                            deviation(ph, t + 1)
                        if m == PAIRS - 1 and "cur" in parts:
                            if "prv" in parts:
                                pool.wait_ge(ph.unit_done, ph.units.through(t, ("wo", 0, 1), parts))
                            residual(ph, t, ph.norm)
                        for unit, part in units_of(m, ph.x_units):
                            if unit[0] == "x" and part in parts:
                                input_lo(t, parts, unit)
                over_batches(pool, B, iteration)

            for ph in passes:
                attention(ph)

            def hidden_lo(t, m):
                pool.wait_ge(ff.u_hi, t * FT + m + 1)
                nc.gpsimd.tensor_tensor(a_lo[:, m, :], hid[:, m % 2, :], f32(a_hi[:, m, :]), ALU.subtract).then_inc(ff.u_lo, 1)

            def iteration(t, parts, parity):
                for m in range(FT):
                    if "cur" in parts:
                        hidden_lo(t, m)
                    if m == 5 and "cur" in parts:
                        at_least(pool, ff.y_done, IT * t)
                        residual(ff, t, 2)
                    if m == 3 and "nxt" in parts:
                        deviation(ff, t + 1)
                    if m == FT - 2 and "nxt" in parts:
                        for k in range(DK):
                            pool.wait_ge(ff.x_mid, DK * (t + 1) + k + 1)
                            nc.gpsimd.tensor_tensor(hT_lo[:, 1 - parity, k, :], hT_full[:, 1 - parity, k, :],
                                                    f32(hT_hi[:, 1 - parity, k, :]), ALU.subtract).then_inc(ff.x_lo, 1)
            over_batches(pool, B, iteration, unroll=2)


_INS = ["x", "ctx_768"] + ["L0_xattn_" + n for n in (
    "ln1_g ln1_b ln2_g ln2_b ln3_g ln3_b sa_wq sa_wk sa_wv sa_wo sa_bo ca_wq ca_wk ca_wv ca_wo ca_bo "
    "ff_w1 ff_b1 ff_w2 ff_b2").split()]


def kernel(**inputs):
    import numpy as _np
    import concourse.bacc as _bacc
    from concourse import mybir as _mybir
    from concourse.bass_utils import run_bass_kernel_spmd as _run

    nc = _bacc.Bacc("TRN2", target_bir_lowering=False, num_devices=1)
    arrays, args = {}, []
    for name in _INS:
        a = _np.ascontiguousarray(inputs[name])
        arrays[f"in_{name}_dram"] = a
        args.append(nc.dram_tensor(f"in_{name}_dram", a.shape, _mybir.dt.from_np(a.dtype), kind="ExternalInput").ap())
    shape = arrays["in_x_dram"].shape
    args.append(nc.dram_tensor("out_dram", shape, F32, kind="ExternalOutput").ap())
    block_kernel(nc, *args)
    r = _run(nc, [arrays], core_ids=[0])
    return r.results[0]["out_dram"]
```

```python
from contextlib import ExitStack

from concourse import mybir

F32 = mybir.dt.float32
F32R = mybir.dt.float32r
ALU = mybir.AluOpType
ACT = mybir.ActivationFunctionType
AX_X = mybir.AxisListType.X

P = 128
D = 256
DK = D // P
S = 256
IT = S // P
H = 16
DH = 64
DA = H * DH
PAIRS = H // 2
HALF = PAIRS // 2
LEAD = 2
RING = 4
T_LAG, O_LAG, A_LAG = 2, 3, 4
X_STEP = PAIRS - LEAD
STAGES = 4
EPS = 1e-5
SCALE = DH ** -0.5
DFF = 4 * D
FT = DFF // P
WCOLS = 2048
FILL, START, STEADY, LAST, DRAIN = ("nxt",), ("cur", "nxt"), ("prv", "cur", "nxt"), ("prv", "cur"), ("prv",)
LEFT, RIGHT = slice(0, DH), slice(DH, 2 * DH)


class Units:

    def __init__(self, x_units, batches):
        self.order = [unit for m in range(PAIRS) for unit in units_of(m, x_units)]
        self.batches = batches
        self.before_loop = self._size(FILL) + self._size(START)
        self.total = self.before_loop + (batches - 2) * len(self.order) + self._size(LAST) + self._size(DRAIN)
        assert len(self.order) % 2 == 0

    def _size(self, parts):
        return sum(part in parts for _, part in self.order)

    def _ahead(self, t, parts):
        if parts in (FILL, START):
            return self._size(FILL) if parts == START else 0
        if parts == DRAIN:
            return self.total - self._size(DRAIN)
        return self.before_loop

    def _place(self, unit, parts):
        return [u for u, part in self.order if part in parts].index(unit)

    def through(self, t, unit, parts):
        n = self._ahead(t, parts) + self._place(unit, parts) + 1
        return (t - 1) * len(self.order) + n if parts in (STEADY, LAST) else n

    def ahead(self, t, parts):
        n = self._ahead(t, parts)
        return (t - 1) * len(self.order) + n if parts in (STEADY, LAST) else n

    def through_qk(self, t, m, parts):
        if m >= LEAD:
            return self.through(t, ("qk", m), parts)
        before = [u for u, part in self.order if part in (FILL if parts == START else STEADY)]
        return self.ahead(t, parts) - (len(before) - before.index(("qk", m)) - 1)

    def bank(self, unit, parts):
        return (self._ahead(None, parts) + self._place(unit, parts)) % 2


def units_of(m, x_units):
    other = [(("v", 0, 1), "cur"), (("wo", 0, 0), "prv"), (("wo", 0, 1), "prv"), (("v", 1, 0), "cur"),
             (("v", 1, 1), "cur"), (("wo", 1, 0), "prv"), (("wo", 1, 1), "prv"), (("v", 0, 0), "nxt")][m]
    qk = (("qk", m + LEAD), "cur") if m < PAIRS - LEAD else (("qk", m + LEAD - PAIRS), "nxt")
    o = (("o", m - O_LAG), "cur") if m >= O_LAG else (("o", m - O_LAG + PAIRS), "prv")
    return [(("x", i), "nxt") for i in range(x_units if m == X_STEP else 0)] + [other, qk, o]


def units_around(m, x_units, in_x_step):
    ahead, before = in_x_step if m == X_STEP else (0, 3) if m == X_STEP - 1 else (0, 2)
    units = units_of(m, x_units)
    return units[:ahead], units[ahead:ahead + before], units[ahead + before:]


def pair_behind(t, m, lag, parts):
    if m >= lag:
        return (t, m - lag) if "cur" in parts else None
    return (t - 1, m - lag + PAIRS) if "prv" in parts else None


def batch_of(t, part):
    return t - 1 if part == "prv" else t if part == "cur" else t + 1


def at_least(eng, sem, value):
    if not (isinstance(value, int) and value <= 0):
        eng.wait_ge(sem, value)


def over_batches(eng, batches, iteration, unroll=1):
    iteration(-1, FILL, 1)
    iteration(0, START, 0)
    with eng.Fori(1, batches - unroll, unroll) as t:
        for i in range(unroll):
            iteration(t + i if i else t, STEADY, (1 + i) % 2)
    iteration(batches - 1, LAST, 1)
    iteration(batches, DRAIN, 0)


def block_kernel(nc, x, ctx, ln1_g, ln1_b, ln2_g, ln2_b, ln3_g, ln3_b, sa_wq, sa_wk, sa_wv, sa_wo, sa_bo,
                 ca_wq, ca_wk, ca_wv, ca_wo, ca_bo, ff_w1, ff_b1, ff_w2, ff_b2, out):
    B = x.shape[0]
    DC = ctx.shape[2]
    stack = ExitStack()
    with stack:
        def sb(name, shape, dt=F32):
            return stack.enter_context(nc.sbuf_tensor(name, shape, dt))

        def psum(name, shape):
            return stack.enter_context(nc.psum_tensor(name, shape, F32))

        def sem(name):
            return stack.enter_context(nc.semaphore(name))

        x_sa = nc.dram_tensor("x_sa_dram", (B, S, D), F32).ap()
        x_ca = nc.dram_tensor("x_ca_dram", (B, S, D), F32).ap()

        s_ps = psum("s_ps", [P, 2, 2, IT * S])
        pt_ps = psum("pt_ps", [P, 2, 2 * S])
        unit_ps = psum("unit_ps", [P, 2, 2 * S])

        w_hi = sb("w_hi", [P, 4, WCOLS], F32R)
        w_lo = sb("w_lo", [P, 4, WCOLS], F32R)
        w_stage = sb("w_stage", [P, STAGES, WCOLS])
        ln_gain = sb("ln_gain", [P, 3, D])
        ln_bias = sb("ln_bias", [P, 3, D])
        b1_col = sb("b1_col", [P, 2 * FT])
        out_bias = sb("out_bias", [P, 3, D])
        ident = sb("ident", [P, P])
        neg_half = sb("neg_half", [P, IT])
        eps = sb("eps", [P, IT])

        x_ln = sb("x_ln", [P, IT, D])
        x_n = sb("x_n", [P, IT, D])
        ctx_in = sb("ctx_in", [P, IT, DK * P])
        x_res = sb("x_res", [P, IT, D])
        x_rb = sb("x_rb", [P, IT, D])
        x_out = sb("x_out", [P, IT, D])
        bn = sb("bn", [P, IT, 6])
        mean_var = sb("mean_var", [P, IT, 2])
        var_eps = sb("var_eps", [P, IT])
        rstd = sb("rstd", [P, IT])
        hT_hi = sb("hT_hi", [P, 2, DK, S], F32R)
        hT_lo = sb("hT_lo", [P, 2, DK, S], F32R)
        qk_hi = sb("qk_hi", [P, RING, 2, S], F32R)
        qk_lo = sb("qk_lo", [P, RING, 2, S], F32R)
        v_hl = sb("v_hl", [P, IT, H, 2 * DH], F32R)
        probs = sb("probs", [P, 2, 2 * IT, S])
        neg_max = sb("neg_max", [P, 2, 2 * IT])
        row_sum = sb("row_sum", [P, 2, 2 * IT])
        row_inv = sb("row_inv", [P, 2, 2 * IT])
        pT_hi = sb("pT_hi", [P, 2, 2, 2 * S], F32R)
        pT_lo = sb("pT_lo", [P, 2, 2, 2 * S], F32R)
        o_lo = sb("o_lo", [DH, 2, 2 * S])
        o_sum = sb("o_sum", [P, 2, S])
        hid = o_sum
        a_hi = sb("a_hi", [P, PAIRS, S], F32R)
        a_lo = sb("a_lo", [P, PAIRS, S], F32R)
        gate = sb("gate", [P, 2, S])

        PARAMS = 16 * 8
        const_ready = sem("const_ready")
        ident_zero = sem("ident_zero")
        norm_ld = sem("norm_ld")
        param_ld = sem("param_ld")
        stage_ld = [sem(f"stage_ld{i}") for i in range(STAGES)]
        w_hi_done = sem("w_hi_done")
        w_done = sem("w_done")

        class NormSemaphores:

            def __init__(self, name):
                self.x_ld = sem(f"{name}_x_ld")
                self.res_ld = sem(f"{name}_res_ld")
                self.stored = sem(f"{name}_stored")
                self.bn_done = sem(f"{name}_bn_done")
                self.stats_done = sem(f"{name}_stats_done")
                self.scaled = sem(f"{name}_scaled")
                self.eps_done = sem(f"{name}_eps_done")
                self.rstd_ready = sem(f"{name}_rstd_ready")
                self.ln_done = sem(f"{name}_ln_done")
                self.x_full = sem(f"{name}_x_full")
                self.x_hi = sem(f"{name}_x_hi")
                self.xrb_done = sem(f"{name}_xrb_done")

        class AttentionPass(NormSemaphores):

            def __init__(self, name, norm, x_in, x_to, has_ctx, weights, w0, before):
                super().__init__(name)
                self.norm, self.x_in, self.x_to, self.weights, self.w0, self.before = norm, x_in, x_to, weights, w0, before
                self.has_ctx = has_ctx
                self.kv = 1 if has_ctx else 0
                self.x_parts = [(0, range(DK)), (1, range(DK))] if has_ctx else [(0, range(k, k + 1)) for k in range(DK)]
                self.units = Units(len(self.x_parts), B)
                self.ctx_ld = sem(f"{name}_ctx_ld")
                self.qk_full = sem(f"{name}_qk_full")
                self.qk_hi = sem(f"{name}_qk_hi")
                self.v_full = sem(f"{name}_v_full")
                self.v_hi = sem(f"{name}_v_hi")
                self.s_full = sem(f"{name}_s_full")
                self.max_done = sem(f"{name}_max_done")
                self.exp_done = sem(f"{name}_exp_done")
                self.inv_done = sem(f"{name}_inv_done")
                self.norm_done = sem(f"{name}_norm_done")
                self.pt_full = sem(f"{name}_pt_full")
                self.pt_hi = sem(f"{name}_pt_hi")
                self.pt_lo = sem(f"{name}_pt_lo")
                self.o_full = sem(f"{name}_o_full")
                self.o_bot = sem(f"{name}_o_bot")
                self.a_hi_done = sem(f"{name}_a_hi_done")
                self.a_done = sem(f"{name}_a_done")
                self.wo_full = sem(f"{name}_wo_full")
                self.unit_done = sem(f"{name}_unit_done")

        class FeedForwardPass(NormSemaphores):

            def __init__(self, name, norm, x_in):
                super().__init__(name)
                self.norm, self.x_in, self.has_ctx = norm, x_in, False
                self.x_lo = sem(f"{name}_x_lo")
                self.p_full = sem(f"{name}_p_full")
                self.gate_done = sem(f"{name}_gate_done")
                self.hid_done = sem(f"{name}_hid_done")
                self.u_hi = sem(f"{name}_u_hi")
                self.u_lo = sem(f"{name}_u_lo")
                self.w2_full = sem(f"{name}_w2_full")
                self.y_done = sem(f"{name}_y_done")

        sa = AttentionPass("sa", 0, x, x_sa, False, [(sa_wq, SCALE), (sa_wk, 1.0), (sa_wv, 1.0), (sa_wo, 1.0)], 0, None)
        ca = AttentionPass("ca", 1, x_sa, x_ca, True, [(ca_wq, SCALE), (ca_wk, 1.0), (ca_wv, 1.0), (ca_wo, 1.0)], 4, sa)
        ff = FeedForwardPass("ff", 2, x_ca)
        passes = (sa, ca)
        after = {sa: ca, ca: ff}

        w1_v = ff_w1.rearrange("(k p) n -> p k n", p=P)
        staged = [(w, scale, slot) for ph in passes for slot, (w, scale) in enumerate(ph.weights)]
        staged += [(w1_v[:, 0, :], 1.0, 0), (w1_v[:, 1, :], 1.0, 1), (ff_w2, 1.0, 2)]

        assert DC - P == P // 2

        def w_pieces(n):
            w = staged[n][0]
            if w.shape[0] == P:
                return [(w, slice(0, P), slice(0, WCOLS))]
            if w.shape[0] == DC:
                last = slice(DA, 2 * DA)
                return [(w[0:P, :], slice(0, P), slice(0, DA)), (w[P:, :], LEFT, last), (w[P:, :], RIGHT, last)]
            return [(w.rearrange("(k p) n -> p k n", p=P), slice(0, P), slice(0, WCOLS))]

        def weights_after(ph):
            return range(ph.w0 + 4, min(ph.w0 + 8, len(staged)))

        def splits(ph, m, parts):
            place = {(FILL, X_STEP): [2], (START, 1): [3]}
            if not ph.before:
                place |= {(FILL, X_STEP - 1): [0], (FILL, X_STEP): [1, 2]}
            return [ph.w0 + n for n in place.get((parts, m), [])]

        def splits_after(ph, m, parts):
            place = {(DRAIN, 0): 0, (DRAIN, A_LAG - 1): 1}.get((parts, m))
            return [] if place is None else [weights_after(ph)[place]]

        def next_norm(ph, t, parts):
            if parts == LAST and ph in after:
                return after[ph], 0
            return (ph, t + 1) if "nxt" in parts and not (parts == FILL and ph is not sa) else None

        def tiles(a):
            return a.rearrange("(i p) d -> p i d", p=P)

        def f32(a):
            return a.bitcast(F32)

        block = stack.enter_context(nc.Block())

        @block.sync
        def _(sp):
            def load_weight(n):
                if n >= STAGES:
                    sp.wait_ge(w_done, n - STAGES + 1)
                for w, rows, cols in w_pieces(n):
                    dst = w_stage[rows, n % STAGES, cols]
                    if len(w.shape) == 3:
                        dst = dst.rearrange("p (k n) -> p k n", k=w.shape[1])
                    sp.dma_start(dst, w).then_inc(stage_ld[n % STAGES], 16)

            def load_inputs(ph, b):
                at_least(sp, ph.ln_done, b)
                sp.dma_start(x_ln[:], tiles(ph.x_in[b])).then_inc(ph.x_ld, 16)
                if ph.has_ctx:
                    at_least(sp, ph.x_full, len(ph.x_parts) * b)
                    sp.dma_start(ctx_in[:, :, 0:DC], tiles(ctx[b])).then_inc(ph.ctx_ld, 16)
                    sp.dma_start(ctx_in[:, :, DC:], tiles(ctx[b])[:, :, P:]).then_inc(ph.ctx_ld, 16)

            def attention(ph):
                def iteration(t, parts, _parity):
                    if parts != FILL and (norm := next_norm(ph, t, parts)):
                        if norm[0] is not ph:
                            sp.wait_ge(ph.ln_done, B)
                        load_inputs(*norm)
                    if parts == START:
                        for n in weights_after(ph):
                            load_weight(n)
                    if "prv" in parts:
                        sp.wait_ge(ph.unit_done, ph.units.through(t, ("wo", 1, 1), parts))
                        sp.dma_start(tiles(ph.x_to[t - 1]), x_out[:]).then_inc(ph.stored, 16)
                        sp.wait_ge(ph.stored, 16 * t)
                    if "cur" in parts:
                        at_least(sp, ph.xrb_done, t)
                        sp.dma_start(x_res[:], tiles(ph.x_in[t])).then_inc(ph.res_ld, 16)
                over_batches(sp, B, iteration)

            def load_norm(i, g, b, landed):
                sp.dma_start(ln_gain[:, i, :], g.unsqueeze(0).broadcast_to([P, D])).then_inc(landed, 16)
                sp.dma_start(ln_bias[:, i, :], b.unsqueeze(0).broadcast_to([P, D])).then_inc(landed, 16)

            load_inputs(sa, 0)
            load_norm(0, ln1_g, ln1_b, norm_ld)
            for n in range(4):
                load_weight(n)
            load_norm(1, ln2_g, ln2_b, param_ld)
            load_norm(2, ln3_g, ln3_b, param_ld)
            sp.dma_start(b1_col[:], ff_b1.rearrange("(k p) -> p k", p=P),
                         allow_slow_non_contiguous=True).then_inc(param_ld, 16)
            for i, b in enumerate((sa_bo, ca_bo, ff_b2)):
                sp.dma_start(out_bias[:, i, :], b.unsqueeze(0).broadcast_to([P, D])).then_inc(param_ld, 16)
            for ph in passes:
                attention(ph)

            def iteration(t, parts, _parity):
                if "nxt" in parts and parts != FILL:
                    load_inputs(ff, t + 1)
                if "prv" in parts:
                    sp.wait_ge(ff.y_done, IT * t)
                    sp.dma_start(tiles(out[t - 1]), x_out[:]).then_inc(ff.stored, 16)
                    sp.wait_ge(ff.stored, 16 * t)
                if "cur" in parts:
                    at_least(sp, ff.xrb_done, t)
                    sp.dma_start(x_res[:], tiles(x_ca[t])).then_inc(ff.res_ld, 16)
            over_batches(sp, B, iteration, unroll=2)
            sp.wait_ge(ff.stored, 16 * B)

        @block.tensor
        def _(pe):
            def three(a_hi, a_lo, b_hi, b_lo):
                return [(a_hi, b_hi), (a_hi, b_lo), (a_lo, b_hi)]

            def product(dst, terms, start=True, stop=True):
                for n, (a, b) in enumerate(terms):
                    last = nc.tensor.matmul(dst, a, b, start=start and n == 0, stop=stop and n == len(terms) - 1)
                return last

            def attention(ph):
                def scores(t, m, parts):
                    g = t * PAIRS + m
                    r = m % RING
                    pe.wait_ge(ph.unit_done, ph.units.through_qk(t, m, parts))
                    at_least(pe, ph.exp_done, g - 1)
                    for it in range(IT):
                        rows = slice(it * P, (it + 1) * P)
                        for n, (q, k) in enumerate(((qk_hi, qk_hi), (qk_hi, qk_lo), (qk_lo, qk_hi))):
                            for hd, part in enumerate((LEFT, RIGHT)):
                                last = nc.tensor.matmul(s_ps[:, m % 2, hd, it * S:(it + 1) * S], q[part, r, 0, rows],
                                                        k[part, r, 1, :], start=n == 0, stop=n == 2)
                    last.then_inc(ph.s_full, 1)

                def transpose_probs(t, m):
                    g = t * PAIRS + m
                    pe.wait_ge(ph.norm_done, g + 1)
                    at_least(pe, ph.pt_lo, g)
                    for hd in range(2):
                        for jt in range(IT):
                            for it in range(IT):
                                last = nc.tensor.transpose(pt_ps[:, hd, jt * S + it * P:jt * S + (it + 1) * P],
                                                           probs[:, m % 2, hd * IT + it, jt * P:(jt + 1) * P], ident[:])
                    last.then_inc(ph.pt_full, 1)

                def projection(slot, cols, side, tokens):
                    terms = []
                    for k in range(DK):
                        w = slice(k * DA + cols.start, k * DA + cols.stop)
                        if side == 1 and k == DK - 1:
                            terms += [(w_hi[:, slot, w], hT_hi[:, side, k, tokens]), (w_lo[LEFT, slot, w], hT_hi[LEFT, side, k, tokens])]
                        else:
                            terms += three(w_hi[:, slot, w], w_lo[:, slot, w], hT_hi[:, side, k, tokens], hT_lo[:, side, k, tokens])
                    return terms

                def run_unit(t, parts, unit, part):
                    b = batch_of(t, part)
                    if unit[0] in ("qk", "v") and part == "nxt":
                        pe.wait_ge(ph.unit_done, ph.units.through(t, ("x", len(ph.x_parts) - 1), parts))
                    bank = unit_ps[:, ph.units.bank(unit, parts), :]
                    at_least(pe, ph.unit_done, ph.units.through(t, unit, parts) - 2)
                    if unit[0] == "qk":
                        m = unit[1]
                        if parts == FILL and m == 0:
                            pe.wait_ge(w_done, ph.w0 + 2)
                        cols = slice(m * P, (m + 1) * P)
                        product(bank[:, 0:S], projection(0, cols, 0, slice(0, S)))
                        product(bank[:, S:2 * S], projection(1, cols, ph.kv, slice(0, S))).then_inc(ph.qk_full, 1)
                    elif unit[0] == "wo":
                        _, half, it = unit
                        pe.wait_ge(ph.a_done, b * PAIRS + (half + 1) * HALF)
                        rows = slice(it * P, (it + 1) * P)
                        product(bank[:, 0:D],
                                [term for m in range(half * HALF, (half + 1) * HALF)
                                 for term in three(a_hi[:, m, rows], a_lo[:, m, rows], w_hi[:, 3, m * D:(m + 1) * D],
                                                   w_lo[:, 3, m * D:(m + 1) * D])]).then_inc(ph.wo_full, 1)
                    elif unit[0] == "o":
                        m = unit[1]
                        pe.wait_ge(ph.pt_lo, b * PAIRS + m + 1)
                        for hd in range(2):
                            for n, (jt, pT) in enumerate((jt, pT) for jt in range(IT) for pT in (pT_hi, pT_lo)):
                                last = nc.tensor.matmul(bank[:, hd * S:(hd + 1) * S], v_hl[:, jt, 2 * m + hd, :],
                                                        pT[:, m % 2, hd, jt * S:(jt + 1) * S], start=n == 0, stop=n == 3)
                        last.then_inc(ph.o_full, 1)
                    elif unit[0] == "v":
                        _, c, jt = unit
                        if parts == FILL and jt == 0:
                            pe.wait_ge(w_done, ph.w0 + 3)
                        rows = slice(jt * P, (jt + 1) * P)
                        cols = slice(c * HALF * P, (c + 1) * HALF * P)
                        product(bank, [(h, w) for w, h in projection(2, cols, ph.kv, rows)]).then_inc(ph.v_full, 1)
                    else:
                        i = unit[1]
                        side, chunks = ph.x_parts[i]
                        if side == 1:
                            pe.wait_ge(ph.ctx_ld, 32 * (b + 1))
                        elif i == 0:
                            pe.wait_ge(ph.ln_done, b + 1)
                        src = (x_n, ctx_in)[side]
                        for n, k in enumerate(chunks):
                            for it in range(IT):
                                last = nc.tensor.transpose(bank[:, n * S + it * P:n * S + (it + 1) * P],
                                                           src[:, it, k * P:(k + 1) * P], ident[:])
                        last.then_inc(ph.x_full, 1)

                def iteration(t, parts, _parity):
                    if parts == FILL and ph.before:
                        pe.wait_ge(ph.before.unit_done, ph.before.units.total)
                    for m in range(PAIRS):
                        ahead, before, behind = units_around(m, len(ph.x_parts), in_x_step=(1, 2))
                        for unit in ahead:
                            if unit[1] in parts:
                                run_unit(t, parts, *unit)
                        if "cur" in parts:
                            scores(t, m, parts)
                        for unit in before:
                            if unit[1] in parts:
                                run_unit(t, parts, *unit)
                        if pair := pair_behind(t, m, T_LAG, parts):
                            transpose_probs(*pair)
                        for unit in behind:
                            if unit[1] in parts:
                                run_unit(t, parts, *unit)
                    if parts == START:
                        pe.wait_ge(w_done, ph.w0 + 4)
                over_batches(pe, B, iteration)

            pe.wait_ge(const_ready, 3)
            for ph in passes:
                attention(ph)

            def hidden(t, m, parity):
                g = t * FT + m
                if m == 0:
                    pe.wait_ge(ff.x_lo, t + 1)
                at_least(pe, ff.hid_done, g - 3)
                for half in range(2):
                    cols = slice(half * DFF + m * P, half * DFF + (m + 1) * P)
                    last = product(s_ps[:, m % 4 // 2, m % 2, half * S:(half + 1) * S],
                                   [term for k in range(DK) for term in three(w_hi[:, k, cols], w_lo[:, k, cols],
                                                                              hT_hi[:, parity, k, :], hT_lo[:, parity, k, :])])
                last.then_inc(ff.p_full, 1)

            def down(b, m):
                pe.wait_ge(ff.u_lo, b * FT + m + 1)
                if m == 0:
                    at_least(pe, ff.y_done, IT * b)
                for it, bank in enumerate((unit_ps[:, 0, :], unit_ps[:, 1, :])):
                    rows = slice(it * P, (it + 1) * P)
                    last = product(bank[:, 0:D], three(a_hi[:, m, rows], a_lo[:, m, rows],
                                                       w_hi[:, 2, m * D:(m + 1) * D], w_lo[:, 2, m * D:(m + 1) * D]),
                                   start=m == 0, stop=m == FT - 1)
                    if m == FT - 1:
                        last.then_inc(ff.w2_full, 1)

            def iteration(t, parts, parity):
                if parts == START:
                    pe.wait_ge(w_done, len(staged) - 1)
                for m in range(FT):
                    if "cur" in parts:
                        hidden(t, m, parity)
                    if m == FT - 2 and "nxt" in parts:
                        pe.wait_ge(ff.ln_done, t + 2)
                        for k in range(DK):
                            for it in range(IT):
                                last = nc.tensor.transpose(pt_ps[:, 0, k * S + it * P:k * S + (it + 1) * P],
                                                           x_n[:, it, k * P:(k + 1) * P], ident[:])
                        last.then_inc(ff.x_full, 1)
                    if m < 2 and "prv" in parts:
                        down(t - 1, m + FT - 2)
                    if m == 2 and parts == START:
                        pe.wait_ge(w_done, len(staged))
                    if m >= 2 and "cur" in parts:
                        down(t, m - 2)
            over_batches(pe, B, iteration, unroll=2)

        @block.scalar
        def _(act):
            def split_weight(n):
                act.wait_ge(stage_ld[n % STAGES], 16 * sum(len(w_pieces(k)) for k in range(n % STAGES, n + 1, STAGES)))
                _, scale, slot = staged[n]
                nc.scalar.activation(w_hi[:, slot, :], w_stage[:, n % STAGES, :], ACT.Copy, scale=scale).then_inc(w_hi_done, 1)

            def attention(ph):
                def split_probs(t, m):
                    act.wait_ge(ph.pt_full, t * PAIRS + m + 1)
                    nc.scalar.copy(pT_hi[:, m % 2, :, :], pt_ps[:]).then_inc(ph.pt_hi, 1)

                def split_heads(t, m, parts):
                    done = ph.units.ahead(t, parts) if m == PAIRS - A_LAG else ph.units.through(t, ("o", m), parts)
                    act.wait_ge(ph.unit_done, done)
                    nc.scalar.copy(a_hi[:, m, :], o_sum[:, m % 2, :]).then_inc(ph.a_hi_done, 1)

                def exponentials(t, m):
                    act.wait_ge(ph.max_done, t * PAIRS + m + 1)
                    for r in range(2 * IT):
                        op = nc.scalar.activation(probs[:, m % 2, r, :], s_ps[:, m % 2, r // IT, r % IT * S:(r % IT + 1) * S],
                                                  ACT.Exp, bias=neg_max[:, m % 2, r:r + 1],
                                                  accum_out=row_sum[:, m % 2, r:r + 1])
                    op.then_inc(ph.exp_done, 1)

                def split_unit(t, parts, unit, part):
                    b = batch_of(t, part)
                    bank = unit_ps[:, ph.units.bank(unit, parts), :]
                    if unit[0] == "qk":
                        act.wait_ge(ph.qk_full, b * PAIRS + unit[1] + 1)
                        nc.scalar.copy(qk_hi[:, unit[1] % RING, :, :],
                                       bank.rearrange("p (a s) -> p a s", a=2)).then_inc(ph.qk_hi, 1)
                    elif unit[0] == "o":
                        act.wait_ge(ph.o_full, b * PAIRS + unit[1] + 1)
                        nc.scalar.copy(o_lo[:, unit[1] % 2, :], bank[DH:P, :]).then_inc(ph.o_bot, 1)
                    elif unit[0] == "v":
                        _, c, jt = unit
                        act.wait_ge(ph.v_full, 4 * b + 2 * c + jt + 1)
                        nc.scalar.copy(v_hl[:, jt, c * PAIRS:(c + 1) * PAIRS, LEFT],
                                       bank.rearrange("p (h d) -> p h d", d=DH)).then_inc(ph.v_hi, 1)
                    elif unit[0] == "x":
                        i = unit[1]
                        side, chunks = ph.x_parts[i]
                        act.wait_ge(ph.x_full, len(ph.x_parts) * b + i + 1)
                        nc.scalar.copy(hT_hi[:, side, chunks.start:chunks.stop, :],
                                       bank[:, 0:len(chunks) * S].rearrange("p (k s) -> p k s", s=S)).then_inc(ph.x_hi, 1)

                def iteration(t, parts, _parity):
                    for m in range(PAIRS):
                        ahead, before, behind = units_around(m, len(ph.x_parts), in_x_step=(2, 1))
                        for i, unit in enumerate(ahead):
                            if unit[1] in parts:
                                split_unit(t, parts, *unit)
                            if i == 0 and (pair := pair_behind(t, m - 1, T_LAG, parts)):
                                split_probs(*pair)
                        if pair := pair_behind(t, m, 1, parts):
                            exponentials(*pair)
                        for i, unit in enumerate(before):
                            if unit[1] in parts:
                                split_unit(t, parts, *unit)
                            if i == 0 and (pair := pair_behind(t, m, A_LAG, parts)):
                                split_heads(t, pair[1], parts)
                        if m != X_STEP - 1 and (pair := pair_behind(t, m, T_LAG, parts)):
                            split_probs(*pair)
                        for n in splits(ph, m, parts):
                            if n == ph.w0 + 3 and ph.before:
                                act.wait_ge(ph.before.unit_done, ph.before.units.total)
                            split_weight(n)
                        for unit in behind:
                            if unit[1] in parts:
                                split_unit(t, parts, *unit)
                        for n in splits_after(ph, m, parts):
                            if m == 0:
                                act.wait_ge(ph.unit_done, ph.units.through(B - 1, ("qk", PAIRS - 1), LAST))
                            split_weight(n)
                over_batches(act, B, iteration)

            for ph in passes:
                attention(ph)
            act.wait_ge(param_ld, PARAMS)

            def gelu(t, m):
                g = t * FT + m
                act.wait_ge(ff.p_full, g + 1)
                at_least(act, ff.hid_done, g - 1)
                nc.scalar.activation(gate[:, m % 2, :], s_ps[:, m % 4 // 2, m % 2, S:2 * S], ACT.Gelu,
                                     bias=b1_col[:, FT + m:FT + m + 1]).then_inc(ff.gate_done, 1)

            def hidden_hi(t, m):
                act.wait_ge(ff.hid_done, t * FT + m + 1)
                nc.scalar.copy(a_hi[:, m, :], hid[:, m % 2, :]).then_inc(ff.u_hi, 1)

            def iteration(t, parts, parity):
                for m in range(FT):
                    if "cur" in parts:
                        gelu(t, m)
                        if m:
                            hidden_hi(t, m - 1)
                        if m == FT - 1:
                            hidden_hi(t, m)
                    if m == FT - 2 and "nxt" in parts:
                        act.wait_ge(ff.x_full, t + 2)
                        nc.scalar.copy(hT_hi[:, 1 - parity, :, :], pt_ps[:, 0, :].rearrange("p (k s) -> p k s", s=S)).then_inc(ff.x_hi, 1)
                        if parts == FILL:
                            split_weight(len(staged) - 1)
            over_batches(act, B, iteration, unroll=2)

        @block.vector
        def _(dve):
            def split_weight(n):
                dve.wait_ge(w_hi_done, n + 1)
                _, scale, slot = staged[n]
                nc.vector.scalar_tensor_tensor(w_lo[:, slot, :], w_stage[:, n % STAGES, :], scale, f32(w_hi[:, slot, :]),
                                               ALU.mult, ALU.subtract).then_inc(w_done, 1)

            def norm_statistics(ph, b):
                dve.wait_ge(ph.x_ld, 16 * (b + 1))
                for it in range(IT):
                    op = nc.vector.bn_stats(bn[:, it, :], x_ln[:, it, :])
                op.then_inc(ph.bn_done, 1)

            def norm_moments(ph, b, first=False):
                for it in range(IT):
                    op = nc.vector.bn_aggr(mean_var[:, it, :], bn[:, it, :])
                op.then_inc(ph.stats_done, 1)
                if first:
                    dve.wait_ge(norm_ld, 16 * 2)
                dve.wait_ge(ph.stats_done, b + 1)
                for it in range(IT):
                    op = nc.vector.scalar_tensor_tensor(x_n[:, it, :], x_ln[:, it, :], mean_var[:, it, 0:1], ln_gain[:, ph.norm, :],
                                                        ALU.subtract, ALU.mult)
                op.then_inc(ph.scaled, 1)

            def normalise(ph, b):
                dve.wait_ge(ph.scaled, b + 1)
                dve.wait_ge(ph.rstd_ready, b + 1)
                for it in range(IT):
                    op = nc.vector.scalar_tensor_tensor(x_n[:, it, :], x_n[:, it, :], rstd[:, it:it + 1], ln_bias[:, ph.norm, :],
                                                        ALU.mult, ALU.add)
                op.then_inc(ph.ln_done, 1)

            def attention(ph):
                def maxima(t, m):
                    dve.wait_ge(ph.s_full, t * PAIRS + m + 1)
                    nc.vector.tensor_reduce(neg_max[:, m % 2, :], s_ps[:, m % 2, :, :].rearrange("p h (i j) -> p (h i) j", j=S),
                                            AX_X, ALU.max, negate=True).then_inc(ph.max_done, 1)

                def invert_sums(t, m):
                    dve.wait_ge(ph.exp_done, t * PAIRS + m + 1)
                    nc.vector.reciprocal(row_inv[:, m % 2, :], row_sum[:, m % 2, :]).then_inc(ph.inv_done, 1)

                def split_probs(t, m):
                    dve.wait_ge(ph.pt_hi, t * PAIRS + m + 1)
                    nc.vector.tensor_tensor(pT_lo[:, m % 2, :, :], pt_ps[:], f32(pT_hi[:, m % 2, :, :]),
                                            ALU.subtract).then_inc(ph.pt_lo, 1)

                def finish_unit(t, parts, unit, part):
                    b = batch_of(t, part)
                    bank = unit_ps[:, ph.units.bank(unit, parts), :]
                    if unit[0] == "qk":
                        r = unit[1] % RING
                        dve.wait_ge(ph.qk_hi, b * PAIRS + unit[1] + 1)
                        op = nc.vector.tensor_tensor(qk_lo[:, r, :, :], bank.rearrange("p (a s) -> p a s", a=2),
                                                     f32(qk_hi[:, r, :, :]), ALU.subtract)
                    elif unit[0] == "o":
                        g = b * PAIRS + unit[1]
                        dve.wait_ge(ph.o_bot, g + 1)
                        at_least(dve, ph.a_done, g - 1)
                        for hd, part in enumerate((LEFT, RIGHT)):
                            cols = slice(hd * S, (hd + 1) * S)
                            op = nc.vector.tensor_tensor(o_sum[part, unit[1] % 2, :], bank[LEFT, cols], o_lo[:, unit[1] % 2, cols], ALU.add)
                    elif unit[0] == "v":
                        _, c, jt = unit
                        dve.wait_ge(ph.v_hi, 4 * b + 2 * c + jt + 1)
                        heads = slice(c * PAIRS, (c + 1) * PAIRS)
                        op = nc.vector.tensor_tensor(v_hl[:, jt, heads, RIGHT], bank.rearrange("p (h d) -> p h d", d=DH),
                                                     f32(v_hl[:, jt, heads, LEFT]), ALU.subtract)
                    elif unit[0] == "x":
                        i = unit[1]
                        side, chunks = ph.x_parts[i]
                        dve.wait_ge(ph.x_hi, len(ph.x_parts) * b + i + 1)
                        for n, k in enumerate(chunks):
                            half = side == 1 and k == DK - 1
                            rows = RIGHT if half else slice(0, P)
                            dst = hT_hi if half else hT_lo
                            op = nc.vector.tensor_tensor(dst[rows, side, k, :], bank[rows, n * S:(n + 1) * S],
                                                         f32(hT_hi[rows, side, k, :]), ALU.subtract)
                    else:
                        _, half, it = unit
                        dve.wait_ge(ph.wo_full, 4 * b + 2 * half + it + 1)
                        if half == 0:
                            dve.wait_ge(ph.xrb_done, b + 1)
                            op = nc.vector.tensor_tensor(x_out[:, it, :], bank[:, 0:D], x_rb[:, it, :], ALU.add)
                        else:
                            dve.wait_ge(ph.unit_done, ph.units.through(t, ("wo", 0, it), parts))
                            op = nc.vector.tensor_tensor(x_out[:, it, :], bank[:, 0:D], x_out[:, it, :], ALU.add)
                    op.then_inc(ph.unit_done, 1)

                def iteration(t, parts, _parity):
                    if parts == START and not ph.before:
                        dve.wait_ge(param_ld, PARAMS)
                    norm = next_norm(ph, t, parts)
                    for m in range(PAIRS):
                        ahead, before, behind = units_around(m, len(ph.x_parts), in_x_step=(2, 1))
                        for i, unit in enumerate(ahead):
                            if unit[1] in parts:
                                finish_unit(t, parts, *unit)
                            if i == 0 and (pair := pair_behind(t, m - 1, T_LAG, parts)):
                                split_probs(*pair)
                        if m == 2 and norm:
                            dve.wait_ge(norm[0].bn_done, norm[1] + 1)
                        if "cur" in parts:
                            maxima(t, m)
                        if pair := pair_behind(t, m, 1, parts):
                            invert_sums(*pair)
                        for i, unit in enumerate(before):
                            if unit[1] in parts:
                                finish_unit(t, parts, *unit)
                            if i == 0 and norm:
                                if m == 1:
                                    norm_statistics(*norm)
                                if m == 2:
                                    norm_moments(*norm, first=parts == FILL)
                                if m == X_STEP - 1:
                                    normalise(*norm)
                        if m != X_STEP - 1 and (pair := pair_behind(t, m, T_LAG, parts)):
                            split_probs(*pair)
                        for n in splits(ph, m, parts):
                            split_weight(n)
                        for unit in behind:
                            if unit[1] in parts:
                                finish_unit(t, parts, *unit)
                        for n in splits_after(ph, m, parts):
                            split_weight(n)
                over_batches(dve, B, iteration)

            for ph in passes:
                attention(ph)

            def gated(t, m):
                g = t * FT + m
                dve.wait_ge(ff.gate_done, g + 1)
                at_least(dve, ff.u_lo, g - 1)
                nc.vector.scalar_tensor_tensor(hid[:, m % 2, :], s_ps[:, m % 4 // 2, m % 2, 0:S], b1_col[:, m:m + 1],
                                               gate[:, m % 2, :], ALU.add, ALU.mult).then_inc(ff.hid_done, 1)

            def iteration(t, parts, parity):
                for m in range(FT):
                    nxt = "nxt" in parts and parts != FILL
                    if m == 3 and nxt:
                        dve.wait_ge(ff.bn_done, t + 2)
                    if "cur" in parts:
                        gated(t, m)
                    if m == 3 and nxt:
                        norm_moments(ff, t + 1)
                    if m == 1 and "prv" in parts:
                        dve.wait_ge(ff.xrb_done, t)
                        for it, bank in enumerate((unit_ps[:, 0, :], unit_ps[:, 1, :])):
                            dve.wait_ge(ff.w2_full, IT * (t - 1) + it + 1)
                            nc.vector.tensor_tensor(x_out[:, it, :], bank[:, 0:D], x_rb[:, it, :], ALU.add).then_inc(ff.y_done, 1)
                    if m == 2 and nxt:
                        norm_statistics(ff, t + 1)
                    if m == 4 and nxt:
                        normalise(ff, t + 1)
                    if m == FT - 2 and "nxt" in parts:
                        dve.wait_ge(ff.x_hi, t + 2)
                        nc.vector.tensor_tensor(hT_lo[:, 1 - parity, :, :], pt_ps[:, 0, :].rearrange("p (k s) -> p k s", s=S),
                                                f32(hT_hi[:, 1 - parity, :, :]), ALU.subtract).then_inc(ff.x_lo, 1)
                        if parts == FILL:
                            split_weight(len(staged) - 1)
            over_batches(dve, B, iteration, unroll=2)

        @block.gpsimd
        def _(pool):
            nc.gpsimd.memset(neg_half[:], -0.5).then_inc(const_ready, 1)
            nc.gpsimd.memset(eps[:], EPS).then_inc(const_ready, 1)
            nc.gpsimd.memset(ident[:], 0.0).then_inc(ident_zero, 1)
            pool.wait_ge(ident_zero, 1)
            nc.gpsimd.affine_select(out=ident[:], in_=ident[:], compare_op=ALU.not_equal, fill=1.0, base=0,
                                    pattern=[[-1, P]], channel_multiplier=1).then_inc(const_ready, 1)
            pool.wait_ge(const_ready, 3)

            def deviation(ph, b):
                pool.wait_ge(ph.stats_done, b + 1)
                nc.gpsimd.tensor_tensor(var_eps[:], mean_var[:, :, 1], eps[:], ALU.add).then_inc(ph.eps_done, 1)
                pool.wait_ge(ph.eps_done, b + 1)
                nc.gpsimd.tensor_tensor(rstd[:], var_eps[:], neg_half[:], ALU.pow).then_inc(ph.rstd_ready, 1)

            def residual(ph, b, bias):
                pool.wait_ge(ph.res_ld, 16 * (b + 1))
                nc.gpsimd.tensor_tensor(x_rb[:], x_res[:], out_bias[:, bias:bias + 1, :].broadcast_to([P, IT, D]),
                                        ALU.add).then_inc(ph.xrb_done, 1)

            def attention(ph):
                def split_heads(b, m):
                    pool.wait_ge(ph.a_hi_done, b * PAIRS + m + 1)
                    nc.gpsimd.tensor_tensor(a_lo[:, m, :], o_sum[:, m % 2, :], f32(a_hi[:, m, :]), ALU.subtract).then_inc(ph.a_done, 1)

                def normalise(t, m):
                    pool.wait_ge(ph.inv_done, t * PAIRS + m + 1)
                    nc.gpsimd.tensor_tensor(probs[:, m % 2, :, :], probs[:, m % 2, :, :],
                                            row_inv[:, m % 2, :].unsqueeze(2).broadcast_to([P, 2 * IT, S]),
                                            ALU.mult).then_inc(ph.norm_done, 1)

                def iteration(t, parts, _parity):
                    for m in range(PAIRS):
                        if pair := pair_behind(t, m, 1, parts):
                            normalise(*pair)
                        if pair := pair_behind(t, m, A_LAG, parts):
                            split_heads(*pair)
                        if m == 0 and parts == START and not ph.before:
                            pool.wait_ge(param_ld, PARAMS)
                        if m == 0 and "prv" in parts:
                            residual(ph, t - 1, ph.norm)
                        if m == 2 and (norm := next_norm(ph, t, parts)):
                            deviation(*norm)
                over_batches(pool, B, iteration)

            for ph in passes:
                attention(ph)

            def hidden_lo(t, m):
                pool.wait_ge(ff.u_hi, t * FT + m + 1)
                nc.gpsimd.tensor_tensor(a_lo[:, m, :], hid[:, m % 2, :], f32(a_hi[:, m, :]), ALU.subtract).then_inc(ff.u_lo, 1)

            def iteration(t, parts, parity):
                for m in range(FT):
                    if "cur" in parts:
                        hidden_lo(t, m)
                    if m == 5 and "cur" in parts:
                        residual(ff, t, 2)
                    if m == 3 and "nxt" in parts and parts != FILL:
                        deviation(ff, t + 1)
            over_batches(pool, B, iteration, unroll=2)


_INS = ["x", "ctx_768"] + ["L0_xattn_" + n for n in (
    "ln1_g ln1_b ln2_g ln2_b ln3_g ln3_b sa_wq sa_wk sa_wv sa_wo sa_bo ca_wq ca_wk ca_wv ca_wo ca_bo "
    "ff_w1 ff_b1 ff_w2 ff_b2").split()]


def kernel(**inputs):
    import numpy as _np
    import concourse.bacc as _bacc
    from concourse import mybir as _mybir
    from concourse.bass_utils import run_bass_kernel_spmd as _run

    nc = _bacc.Bacc("TRN2", target_bir_lowering=False, num_devices=1)
    arrays, args = {}, []
    for name in _INS:
        a = _np.ascontiguousarray(inputs[name])
        arrays[f"in_{name}_dram"] = a
        args.append(nc.dram_tensor(f"in_{name}_dram", a.shape, _mybir.dt.from_np(a.dtype), kind="ExternalInput").ap())
    shape = arrays["in_x_dram"].shape
    args.append(nc.dram_tensor("out_dram", shape, F32, kind="ExternalOutput").ap())
    block_kernel(nc, *args)
    r = _run(nc, [arrays], core_ids=[0])
    return r.results[0]["out_dram"]
```
